# Optimizing a Trainium2 kernel written in Bass

```python
import numpy as np
import jax
import jax.numpy as jnp

def _softmax(x, axis=-1):
    return jax.nn.softmax(x, axis=axis)

def _gelu(x):
    return jax.nn.gelu(x, approximate=True)

def _silu(x):
    return jax.nn.silu(x)

def _sigmoid(x):
    return jax.nn.sigmoid(x)

def _layernorm(x, axis=-1, eps=1e-05):
    m = jnp.mean(x, axis=axis, keepdims=True)
    v = jnp.var(x, axis=axis, keepdims=True)
    return (x - m) / jnp.sqrt(v + eps)

def _scatter_add(tgt, idx, src, axis=0):
    return tgt.at[idx].add(src)

def _segment_sum(src, seg, n):
    return jax.ops.segment_sum(src, seg, n)
kernel_name = 'mk_xattn_seq_d2_seqx_r8_79c055'

def setup_inputs(seed: int=0):
    np.random.seed(seed)
    _w = jnp.asarray

    def _rec_inputs():
        import jax
        import jax.numpy as jnp
        _rk = jax.random.key(seed)
        x = -0.0002928 + 1 * jax.random.normal(jax.random.fold_in(_rk, 1), (64, 64, 256), jnp.float32)
        _lenS = 64 - jax.random.randint(jax.random.fold_in(_rk, 7), (64,), 0, max(1, 64 // 4) + 1, jnp.int32)
        _lenS2 = 64 - jax.random.randint(jax.random.fold_in(_rk, 8), (64,), 0, max(1, 64 // 4) + 1, jnp.int32)
        _ctx_2048P = jax.random.normal(jax.random.fold_in(_rk, 11), (64, 16, 256), jnp.float32)
        _ctx_2048c = jax.random.dirichlet(jax.random.fold_in(_rk, 511), 0.3 * jnp.ones((16,), jnp.float32), (64, 64))
        _ctx_2048t = jnp.einsum('bsk,bkd->bsd', _ctx_2048c, _ctx_2048P)
        _ctx_2048t = _ctx_2048t * jax.lax.rsqrt(jnp.mean(jnp.square(_ctx_2048t)) + 1e-12) * 0.953939
        ctx_2048 = -1.39393e-06 + 0.999914 * (_ctx_2048t + 0.3 * jax.random.normal(jax.random.fold_in(_rk, 611), (64, 64, 256), jnp.float32))
        _validS = jnp.arange(64)[None, :] < _lenS[:, None]
        _validS2 = jnp.arange(64)[None, :] < _lenS2[:, None]
        _causal = jnp.tril(jnp.ones((64, 64), dtype=bool))
        mask_1x1xSxS2_fc1 = jnp.where(jnp.broadcast_to(_validS2[0:1, None, None, :], (1, 1, 64, 64)), 1.0, 0.0).astype(jnp.float32)
        mask_Bx1xSxS2_ff1 = jnp.where(jnp.ones((64, 1, 64, 64), dtype=bool), 1.0, 0.0).astype(jnp.float32)
        mask_BxS2_ik0 = jnp.where(jnp.broadcast_to(_validS2[:, :], (64, 64)), 0, 1).astype(jnp.int32)
        return (x, ctx_2048, mask_1x1xSxS2_fc1, mask_Bx1xSxS2_ff1, mask_BxS2_ik0)
    x, ctx_2048, mask_1x1xSxS2_fc1, mask_Bx1xSxS2_ff1, mask_BxS2_ik0 = _rec_inputs()

    def _L0_xattn_setup():
        import jax, jax.numpy as jnp
        import numpy as np
        H = 256
        NH = 16
        HD = H // NH
        EPS = 1e-05

        def gelu(x):
            return 0.5 * x * (1.0 + jnp.tanh(0.7978845608028654 * x * (1.0 + 0.044715 * x * x)))

        def layernorm(x, scale, bias):
            m = jnp.mean(x, axis=-1, keepdims=True)
            v = jnp.mean(jnp.square(x - m), axis=-1, keepdims=True)
            return (x - m) * jax.lax.rsqrt(v + EPS) * scale + bias

        def split_heads(x):
            b, s, _ = x.shape
            return x.reshape(b, s, NH, HD).transpose(0, 2, 1, 3)

        def merge_heads(x):
            b, nh, s, hd = x.shape
            return x.transpose(0, 2, 1, 3).reshape(b, s, nh * hd)

        def attention(q, k, v, mask):
            scores = jnp.einsum('bhqd,bhkd->bhqk', q, k) / jnp.sqrt(jnp.float32(HD))
            scores = scores * mask - 10000.0 * (1.0 - mask)
            probs = jax.nn.softmax(scores, axis=-1)
            return jnp.einsum('bhqk,bhkd->bhqd', probs, v)
        key = jax.random.key(seed)
        ks = jax.random.split(key, 16)
        b, s, t = (2, 128, 128)
        w = lambda k, i, o: jax.random.normal(k, (i, o), jnp.float32) * 0.02
        inp = {'hidden_states': jax.random.normal(ks[0], (b, s, H), jnp.float32), 'encoder_states': jax.random.normal(ks[1], (b, t, H), jnp.float32), 'ltor_mask': jnp.tril(jnp.ones((1, 1, s, s), jnp.float32)), 'cross_mask': jnp.ones((b, 1, s, t), jnp.float32), 'ln1_s': jnp.ones((H,), jnp.float32), 'ln1_b': jnp.zeros((H,), jnp.float32), 'w_qkv': w(ks[2], H, 3 * H), 'b_qkv': jnp.zeros((3 * H,), jnp.float32), 'w_ao': w(ks[3], H, H), 'b_ao': jnp.zeros((H,), jnp.float32), 'ln2_s': jnp.ones((H,), jnp.float32), 'ln2_b': jnp.zeros((H,), jnp.float32), 'w_q': w(ks[4], H, H), 'b_q': jnp.zeros((H,), jnp.float32), 'w_kv': w(ks[5], H, 2 * H), 'b_kv': jnp.zeros((2 * H,), jnp.float32), 'w_co': w(ks[6], H, H), 'b_co': jnp.zeros((H,), jnp.float32), 'ln3_s': jnp.ones((H,), jnp.float32), 'ln3_b': jnp.zeros((H,), jnp.float32), 'w1': w(ks[7], H, 4 * H), 'b1': jnp.zeros((4 * H,), jnp.float32), 'w2': w(ks[8], 4 * H, H), 'b2': jnp.zeros((H,), jnp.float32)}
        return inp
    _L0_xattn_all = _L0_xattn_setup()
    _L0_xattn_in = {k: v for k, v in _L0_xattn_all.items() if k in ('ln1_s', 'ln1_b', 'w_qkv', 'b_qkv', 'w_ao', 'b_ao', 'ln2_s', 'ln2_b', 'w_q', 'b_q', 'w_kv', 'b_kv', 'w_co', 'b_co', 'ln3_s', 'ln3_b', 'w1', 'b1', 'w2', 'b2')}
    del _L0_xattn_all

    def _L1_xattn_setup():
        import jax, jax.numpy as jnp
        import numpy as np
        B, P, K, H, NH = (4, 256, 32, 256, 16)
        DH = H // NH
        EPS = 1e-06

        def rmsnorm(x, w):
            var = jnp.mean(jnp.square(x), axis=-1, keepdims=True)
            return x * jax.lax.rsqrt(var + EPS) * w
        key = jax.random.key(seed)
        ks = jax.random.split(key, 12)
        s = 0.02
        return {'x': jax.random.normal(ks[0], (B, P, H), jnp.float32), 'latents': jax.random.normal(ks[1], (B, K, H), jnp.float32), 'attention_mask': jax.random.randint(ks[2], (B, P), 0, 2, jnp.int32), 'q_w': s * jax.random.normal(ks[3], (H, H), jnp.float32), 'q_b': jnp.zeros((H,), jnp.float32), 'kv_w': s * jax.random.normal(ks[4], (H, 2 * H), jnp.float32), 'kv_b': jnp.zeros((2 * H,), jnp.float32), 'out_w': s * jax.random.normal(ks[5], (H, H), jnp.float32), 'out_b': jnp.zeros((H,), jnp.float32), 'postnorm_w': jnp.ones((H,), jnp.float32), 'mlp_w1': s * jax.random.normal(ks[6], (H, 4 * H), jnp.float32), 'mlp_b1': jnp.zeros((4 * H,), jnp.float32), 'mlp_w2': s * jax.random.normal(ks[7], (4 * H, H), jnp.float32), 'mlp_b2': jnp.zeros((H,), jnp.float32)}
    _L1_xattn_all = _L1_xattn_setup()
    _L1_xattn_in = {k: v for k, v in _L1_xattn_all.items() if k in ('q_w', 'q_b', 'kv_w', 'kv_b', 'out_w', 'out_b', 'postnorm_w', 'mlp_w1', 'mlp_b1', 'mlp_w2', 'mlp_b2')}
    del _L1_xattn_all
    return {'x': x, 'ctx_2048': ctx_2048, 'mask_1x1xSxS2_fc1': mask_1x1xSxS2_fc1, 'mask_Bx1xSxS2_ff1': mask_Bx1xSxS2_ff1, 'mask_BxS2_ik0': mask_BxS2_ik0, 'L0_xattn_ln1_s': _L0_xattn_in['ln1_s'], 'L0_xattn_ln1_b': _L0_xattn_in['ln1_b'], 'L0_xattn_w_qkv': _L0_xattn_in['w_qkv'], 'L0_xattn_b_qkv': _L0_xattn_in['b_qkv'], 'L0_xattn_w_ao': _L0_xattn_in['w_ao'], 'L0_xattn_b_ao': _L0_xattn_in['b_ao'], 'L0_xattn_ln2_s': _L0_xattn_in['ln2_s'], 'L0_xattn_ln2_b': _L0_xattn_in['ln2_b'], 'L0_xattn_w_q': _L0_xattn_in['w_q'], 'L0_xattn_b_q': _L0_xattn_in['b_q'], 'L0_xattn_w_kv': _L0_xattn_in['w_kv'], 'L0_xattn_b_kv': _L0_xattn_in['b_kv'], 'L0_xattn_w_co': _L0_xattn_in['w_co'], 'L0_xattn_b_co': _L0_xattn_in['b_co'], 'L0_xattn_ln3_s': _L0_xattn_in['ln3_s'], 'L0_xattn_ln3_b': _L0_xattn_in['ln3_b'], 'L0_xattn_w1': _L0_xattn_in['w1'], 'L0_xattn_b1': _L0_xattn_in['b1'], 'L0_xattn_w2': _L0_xattn_in['w2'], 'L0_xattn_b2': _L0_xattn_in['b2'], 'L1_xattn_q_w': _L1_xattn_in['q_w'], 'L1_xattn_q_b': _L1_xattn_in['q_b'], 'L1_xattn_kv_w': _L1_xattn_in['kv_w'], 'L1_xattn_kv_b': _L1_xattn_in['kv_b'], 'L1_xattn_out_w': _L1_xattn_in['out_w'], 'L1_xattn_out_b': _L1_xattn_in['out_b'], 'L1_xattn_postnorm_w': _L1_xattn_in['postnorm_w'], 'L1_xattn_mlp_w1': _L1_xattn_in['mlp_w1'], 'L1_xattn_mlp_b1': _L1_xattn_in['mlp_b1'], 'L1_xattn_mlp_w2': _L1_xattn_in['mlp_w2'], 'L1_xattn_mlp_b2': _L1_xattn_in['mlp_b2']}

def reference(x, ctx_2048, mask_1x1xSxS2_fc1, mask_Bx1xSxS2_ff1, mask_BxS2_ik0, L0_xattn_ln1_s, L0_xattn_ln1_b, L0_xattn_w_qkv, L0_xattn_b_qkv, L0_xattn_w_ao, L0_xattn_b_ao, L0_xattn_ln2_s, L0_xattn_ln2_b, L0_xattn_w_q, L0_xattn_b_q, L0_xattn_w_kv, L0_xattn_b_kv, L0_xattn_w_co, L0_xattn_b_co, L0_xattn_ln3_s, L0_xattn_ln3_b, L0_xattn_w1, L0_xattn_b1, L0_xattn_w2, L0_xattn_b2, L1_xattn_q_w, L1_xattn_q_b, L1_xattn_kv_w, L1_xattn_kv_b, L1_xattn_out_w, L1_xattn_out_b, L1_xattn_postnorm_w, L1_xattn_mlp_w1, L1_xattn_mlp_b1, L1_xattn_mlp_w2, L1_xattn_mlp_b2):
    import jax
    import jax.numpy as jnp

    def _L0_xattn_ref(hidden_states, encoder_states, ltor_mask, cross_mask, ln1_s, ln1_b, w_qkv, b_qkv, w_ao, b_ao, ln2_s, ln2_b, w_q, b_q, w_kv, b_kv, w_co, b_co, ln3_s, ln3_b, w1, b1, w2, b2):
        import jax, jax.numpy as jnp
        import numpy as np
        H = 256
        NH = 16
        HD = H // NH
        EPS = 1e-05

        def gelu(x):
            return 0.5 * x * (1.0 + jnp.tanh(0.7978845608028654 * x * (1.0 + 0.044715 * x * x)))

        def layernorm(x, scale, bias):
            m = jnp.mean(x, axis=-1, keepdims=True)
            v = jnp.mean(jnp.square(x - m), axis=-1, keepdims=True)
            return (x - m) * jax.lax.rsqrt(v + EPS) * scale + bias

        def split_heads(x):
            b, s, _ = x.shape
            return x.reshape(b, s, NH, HD).transpose(0, 2, 1, 3)

        def merge_heads(x):
            b, nh, s, hd = x.shape
            return x.transpose(0, 2, 1, 3).reshape(b, s, nh * hd)

        def attention(q, k, v, mask):
            scores = jnp.einsum('bhqd,bhkd->bhqk', q, k) / jnp.sqrt(jnp.float32(HD))
            scores = scores * mask - 10000.0 * (1.0 - mask)
            probs = jax.nn.softmax(scores, axis=-1)
            return jnp.einsum('bhqk,bhkd->bhqd', probs, v)
        ln_out = layernorm(hidden_states, ln1_s, ln1_b)
        qkv = ln_out @ w_qkv + b_qkv
        q, k, v = jnp.split(qkv, 3, axis=-1)
        ctx = merge_heads(attention(split_heads(q), split_heads(k), split_heads(v), ltor_mask))
        attn_out = ctx @ w_ao + b_ao
        x = hidden_states + attn_out
        ln_out = layernorm(x, ln2_s, ln2_b)
        q = ln_out @ w_q + b_q
        kv = encoder_states @ w_kv + b_kv
        k, v = jnp.split(kv, 2, axis=-1)
        ctx = merge_heads(attention(split_heads(q), split_heads(k), split_heads(v), cross_mask))
        cross_out = ctx @ w_co + b_co
        x = x + cross_out
        ln_out = layernorm(x, ln3_s, ln3_b)
        mlp_out = gelu(ln_out @ w1 + b1) @ w2 + b2
        return x + mlp_out

    def _L1_xattn_ref(x, latents, attention_mask, q_w, q_b, kv_w, kv_b, out_w, out_b, postnorm_w, mlp_w1, mlp_b1, mlp_w2, mlp_b2):
        import jax, jax.numpy as jnp
        import numpy as np
        B, P, K, H, NH = (4, 256, 32, 256, 16)
        DH = H // NH
        EPS = 1e-06

        def rmsnorm(x, w):
            var = jnp.mean(jnp.square(x), axis=-1, keepdims=True)
            return x * jax.lax.rsqrt(var + EPS) * w
        b, p, _ = x.shape
        k_len = latents.shape[1]
        residual = latents
        h = jnp.concatenate([x, latents], axis=1)
        q = (latents @ q_w + q_b).reshape(b, k_len, NH, DH)
        kv = (h @ kv_w + kv_b).reshape(b, p + k_len, NH, DH, 2)
        kmat, v = (kv[..., 0], kv[..., 1])
        attn = jnp.einsum('bkhd,bnhd->bhkn', q, kmat) / DH
        full_mask = jnp.concatenate([attention_mask.astype(bool), jnp.ones((b, k_len), bool)], axis=-1)
        attn = jnp.where(full_mask[:, None, None, :], attn, -jnp.inf)
        attn = jax.nn.softmax(attn.astype(jnp.float32), axis=-1).astype(q.dtype)
        attn_out = jnp.einsum('bhkn,bnhd->bkhd', attn, v).reshape(b, k_len, H)
        attn_out = attn_out @ out_w + out_b + residual
        out = rmsnorm(attn_out, postnorm_w)
        out = jax.nn.gelu(out @ mlp_w1 + mlp_b1) @ mlp_w2 + mlp_b2
        return out + residual
    x = _L0_xattn_ref(x, ctx_2048, mask_1x1xSxS2_fc1, mask_Bx1xSxS2_ff1, L0_xattn_ln1_s, L0_xattn_ln1_b, L0_xattn_w_qkv, L0_xattn_b_qkv, L0_xattn_w_ao, L0_xattn_b_ao, L0_xattn_ln2_s, L0_xattn_ln2_b, L0_xattn_w_q, L0_xattn_b_q, L0_xattn_w_kv, L0_xattn_b_kv, L0_xattn_w_co, L0_xattn_b_co, L0_xattn_ln3_s, L0_xattn_ln3_b, L0_xattn_w1, L0_xattn_b1, L0_xattn_w2, L0_xattn_b2)
    x = _L1_xattn_ref(ctx_2048, x, mask_BxS2_ik0, L1_xattn_q_w, L1_xattn_q_b, L1_xattn_kv_w, L1_xattn_kv_b, L1_xattn_out_w, L1_xattn_out_b, L1_xattn_postnorm_w, L1_xattn_mlp_w1, L1_xattn_mlp_b1, L1_xattn_mlp_w2, L1_xattn_mlp_b2)
    return x

_drawn_inputs = setup_inputs


def setup_inputs(seed=0):
    import zlib

    import numpy as np

    out = dict(_drawn_inputs(seed))
    spreads = {'L0_xattn_ln1_s': (1.0, 0.6),
     'L0_xattn_ln1_b': (0.0, 0.773),
     'L0_xattn_b_qkv': (0.0, 0.277),
     'L0_xattn_b_ao': (0.0, 0.1),
     'L0_xattn_ln2_s': (1.0, 0.6),
     'L0_xattn_ln2_b': (0.0, 2.0),
     'L0_xattn_b_q': (0.0, 2.0),
     'L0_xattn_b_kv': (0.0, 0.286),
     'L0_xattn_b_co': (0.0, 0.1),
     'L0_xattn_ln3_s': (1.0, 0.6),
     'L0_xattn_ln3_b': (0.0, 0.665),
     'L0_xattn_b1': (0.0, 0.1),
     'L0_xattn_b2': (0.0, 0.1),
     'L1_xattn_q_b': (0.0, 0.8),
     'L1_xattn_kv_b': (0.0, 0.8),
     'L1_xattn_out_b': (0.0, 2.0),
     'L1_xattn_postnorm_w': (1.0, 0.6),
     'L1_xattn_mlp_b1': (0.0, 0.1),
     'L1_xattn_mlp_b2': (0.0, 0.1)}
    factors = {'L0_xattn_w_qkv': 3.137,
     'L0_xattn_w_q': 8.0,
     'L1_xattn_q_w': 8.0,
     'L1_xattn_kv_w': 8.0,
     'L1_xattn_out_w': 8.0}
    for name, (base, spread) in spreads.items():
        noise = np.random.default_rng([zlib.crc32(name.encode()), seed]).standard_normal(out[name].shape)
        drawn = base * np.exp(spread * noise) if base else spread * noise
        out[name] = jnp.asarray(drawn.astype(out[name].dtype))
    for name, factor in factors.items():
        out[name] = (out[name] * factor).astype(out[name].dtype)
    return out
```

```python
from contextlib import ExitStack

import numpy as np

import concourse.bass as bass
from concourse import mybir

F32 = mybir.dt.float32
I32 = mybir.dt.int32
ALU = mybir.AluOpType
ACT = mybir.ActivationFunctionType
AX = mybir.AxisListType

P = 128
B, S, H = 64, 64, 256
NH = 16
HD = H // NH
KH = H // P
HB = P // HD
NP = NH // 2
FF = 4 * H
NF = FF // P
BU = P // S
UNITS = B // BU
STREAMS = 3
VW = 2 * (HD + 1)
L0_EPS, L1_EPS = 1e-5, 1e-6
L0_SCALE = float(HD) ** -0.5
L1_SCALE = 1.0 / HD
MASKED = -1e30

COLS = {}
for _name, _n in (("ln1_s", 2), ("ln1_b", 2), ("b_qkv", 6), ("ln2_s", 2), ("ln2_b", 2), ("b_q", 2),
                  ("b_kv", 4), ("ln3_s", 2), ("ln3_b", 2), ("b1", 8), ("q_b", 2), ("k_b", 2),
                  ("v_b", 2), ("postnorm_w", 2), ("mlp_b1", 8)):
    COLS[_name] = (sum(n for _, n in COLS.values()), _n)
NCOLS = sum(n for _, n in COLS.values())
ROWS = {n: i for i, n in enumerate(("b_ao", "b_co", "b2", "out_b", "mlp_b2"))}


class Step:

    def __init__(self, engine, ns, name, after, emit, dmas=0):
        self.engine, self.ns, self.name, self.emit, self.dmas = engine, ns, name, emit, dmas
        self.after = [k for k in after if k is not None]


class Take:
    def __init__(self, pool):
        self.pool = pool


class Plan:

    def __init__(self, nc, ctx):
        self.nc, self.ctx = nc, ctx
        self.queues = {e: [] for e in ("sync", "gpsimd", "scalar", "vector", "tensor")}
        self.sems, self.count, self.value, self.owner = {}, {}, {}, {}
        self.waited = {e: {} for e in self.queues}
        self.engine_free = {e: 0.0 for e in self.queues}
        self.at = {}
        self.pools = {}

    def add(self, step):
        kind = step.name[0]
        assert self.owner.setdefault(kind, step.engine) == step.engine, kind
        if kind not in self.sems:
            self.sems[kind] = self.ctx.enter_context(self.nc.semaphore("s_" + kind))
            self.count[kind] = 0
        waits = []
        for key in step.after:
            v = self.value[key]
            if self.waited[step.engine].get(key[0], 0) < v:
                self.waited[step.engine][key[0]] = v
                waits.append((self.sems[key[0]], v))
        dmas = step.dmas
        self.count[kind] += 16 * dmas if dmas else 1
        self.value[step.name] = self.count[kind]
        sem = self.sems[kind]

        def run(eng):
            for s, v in waits:
                eng.wait_ge(s, v)
            last = step.emit(eng)
            if dmas:
                assert len(last) == dmas
                for i in last:
                    i.then_inc(sem, 16)
            else:
                last.then_inc(sem, 1)
        self.queues[step.engine].append(run)
        start = self.start(step)
        self.engine_free[step.engine] = start + (60 * dmas if dmas else step.ns)
        self.at[step.name] = start + step.ns + (2200 if dmas else 200)

    def start(self, step):
        return max([self.engine_free[step.engine]] + [self.at[k] for k in step.after])

    def known(self, step):
        return all(k in self.value for k in step.after)

    def pool(self, name, slots):
        self.pools[name] = [(i, None) for i in range(slots)]

    def free(self, name, slot, key):
        self.pools[name].append((slot, key))

    def weave(self, streams):
        heads = [(next(s), s) for s in streams]
        while heads:
            best = None
            for n, (head, s) in enumerate(heads):
                while isinstance(head, Take) and self.pools[head.pool]:
                    head = s.send(self.pools[head.pool].pop(0))
                    heads[n] = (head, s)
                if isinstance(head, Take) or not self.known(head):
                    continue
                t = self.start(head)
                if best is None or t < best[0] - 50:
                    best = (t, n)
            assert best is not None, [h.pool if isinstance(h, Take) else (h.name, h.after) for h, _ in heads]
            head, s = heads[best[1]]
            self.add(head)
            try:
                heads[best[1]] = (next(s), s)
            except StopIteration:
                del heads[best[1]]


def build(nc, x_in, ctxT_in, mask_self_in, mask_cross_in, mask_keys_in, cols_in, rows_in, weights_in,
          out):
    with ExitStack() as ctx:
        def sb(name, shape, dt=F32):
            return ctx.enter_context(nc.sbuf_tensor(name, shape, dt))

        plan = Plan(nc, ctx)

        scores = [ctx.enter_context(nc.psum_tensor(f"scores{i}", [P, NH * S], F32)) for i in range(2)]
        work = [ctx.enter_context(nc.psum_tensor(f"work{i}", [P, 512], F32)) for i in range(3)]
        mixed = [ctx.enter_context(nc.psum_tensor("mixed", [P, 512], F32))]
        plan.pool("scores", 2)
        plan.pool("work", 3)
        plan.pool("mixed", 1)

        w = {name: sb("w_" + name, [P, ap.shape[0] // P, ap.shape[1]]) for name, ap in weights_in.items()}
        cols = sb("cols", [P, NCOLS])
        rows = sb("rows", [P, len(ROWS), H])
        folded = sb("folded", [P, 16])
        spread_bias = sb("spread_bias", [P, KH, P])
        ident = sb("ident", [P, P])
        minus_half = sb("minus_half", [P, 1])
        mask_self = sb("mask_self", [P, S])
        add_self = sb("add_self", [P, S])
        mask_keys_i = sb("mask_keys_i", [P, UNITS, S], I32)
        mask_keys = mask_keys_i[:, :, :].bitcast(F32)

        NKEYS = 4
        spread = [sb(f"spread{i}", [P, KH, HB, P]) for i in range(NKEYS)]
        plan.pool("spread", NKEYS)

        class Buffers:
            pass

        bufs = []
        for s in range(STREAMS):
            b = Buffers()
            b.x = sb(f"x{s}", [P, H])
            b.xb = sb(f"xb{s}", [P, H])
            b.xn = sb(f"xn{s}", [P, H])
            b.xT = sb(f"xT{s}", [P, KH, P])
            b.ctxT = sb(f"ctxT{s}", [P, KH, P])
            b.qk = sb(f"qk{s}", [P, 2 * KH, P])
            b.kc = sb(f"kc{s}", [P, KH, P])
            b.prob = [sb(f"prob{s}_{i}", [P, NH, S]) for i in range(2)]
            b.hid = b.prob[0][:, :, :].rearrange("p (f a) k -> p f (a k)", f=NF)
            b.probT = sb(f"probT{s}", [P, 2 * NP, P])
            b.val = [sb(f"val{s}_{i}", [P, BU, NP, VW]) for i in range(2)]
            b.mask = sb(f"mask{s}", [P, S])
            b.add = sb(f"add{s}", [P, S])
            b.bn = sb(f"bn{s}", [P, 6])
            b.mv = sb(f"mv{s}", [P, 2])
            b.var = sb(f"var{s}", [P, 1])
            b.rstd = sb(f"rstd{s}", [P, 1])
            b.mx = [sb(f"mx{s}_{i}", [P, NH]) for i in range(2)]
            b.rs = sb(f"rs{s}", [P, NH])
            bufs.append(b)

        def col(name, i=0, n=1):
            c = COLS[name][0] + i
            return cols[:, c:c + n]

        def step(engine, ns, name, after, emit):
            return Step(engine, ns, name, after, emit)

        def dma(name, after, pairs):
            return Step("sync", 0, name, after, lambda eng: [eng.dma_start(o, i) for o, i in pairs],
                        dmas=len(pairs))

        def setup():
            yield dma(("ld_cols",), [], [(cols[:, :], cols_in)])
            yield dma(("ld_w_qkv",), [], [(w["qkv"][:, :, :], weights_in["qkv"].rearrange("(k p) n -> p k n", p=P))])
            for name in ("ao", "q", "kv", "co", "m1", "m2", "lq", "lk", "lv", "lo", "n1", "n2"):
                if name == "q":
                    yield dma(("ld_rows",), [], [(rows[:, :, :], rows_in.broadcast_to([P, len(ROWS), H]))])
                    yield dma(("ld_mask_self",), [], [(mask_self[S * b:S * b + S, :], mask_self_in) for b in range(BU)])
                yield dma((f"ld_w_{name}",), [], [(w[name][:, :, :], weights_in[name].rearrange("(k p) n -> p k n", p=P))])
            yield dma(("ld_mask_keys",), [],
                      [(mask_keys_i[S * b:S * b + S, :, :],
                        mask_keys_in.rearrange("(u b) k -> b u k", b=BU)[b:b + 1].broadcast_to([S, UNITS, S]))
                       for b in range(BU)])

        def constants():
            yield step("gpsimd", 200, ("ident0",), [], lambda e: e.memset(ident[:, :], 0.0))
            yield step("gpsimd", 200, ("ident",), [("ident0",)],
                       lambda e: e.affine_select(out=ident[:, :], in_=ident[:, :], compare_op=ALU.not_equal,
                                                 fill=1.0, base=0, pattern=[[-1, P]], channel_multiplier=1))
            yield step("gpsimd", 100, ("minus_half",), [], lambda e: e.memset(minus_half[:, :], -0.5))
            for s in range(STREAMS):
                for i in range(2):
                    v = bufs[s].val[i]
                    yield step("vector", 600, ("val0", s, i), [], lambda e, v=v: e.memset(v[:, :, :, :], 0.0))

                    def ones(e, v=v):
                        for half in range(2):
                            last = e.memset(v[S * half:S * half + S, :, :, half * (HD + 1) + HD:half * (HD + 1) + HD + 1], 1.0)
                        return last
                    yield step("vector", 200, ("val1", s, i), [("val0", s, i)], ones)
            for i in range(NKEYS):
                yield step("gpsimd", 2200, ("spread0", i), [], lambda e, i=i: e.memset(spread[i][:, :, :, :], 0.0))

        def fold(name, wname, first, tiles, beta, at, bias, scale):
            slot, free = yield Take("work")

            def products(e):
                for f in range(tiles):
                    for k in range(KH):
                        last = e.matmul(work[slot][:, f:f + 1], w[wname][:, k, (first + f) * P:(first + f + 1) * P],
                                        col(beta, k), start=(k == 0), stop=(k == KH - 1))
                return last
            yield step("tensor", 900 * tiles, ("fold_mm", name), [("ld_w_" + wname,), ("ld_cols",), free], products)
            yield step("vector", 100, ("fold_add", name), [("fold_mm", name)],
                       lambda e: e.tensor_tensor(folded[:, at:at + tiles], work[slot][:, 0:tiles],
                                                 col(bias[0], bias[1], tiles), ALU.add))
            plan.free("work", slot, ("fold_add", name))
            if scale != 1.0:
                yield step("vector", 100, ("fold_add", name, 1), [("fold_add", name)],
                           lambda e: e.tensor_scalar(folded[:, at:at + tiles], folded[:, at:at + tiles],
                                                     scale, None, ALU.mult))

        def scale_rows(key, wname, lo, hi, s_col, scale, after):
            def emit(e):
                for k in range(KH):
                    a = w[wname][:, k, lo:hi]
                    if s_col is None:
                        last = e.tensor_scalar(a, a, scale, None, ALU.mult)
                    else:
                        last = e.tensor_scalar(a, a, col(s_col, k), scale, ALU.mult, ALU.mult)
                return last
            return step("vector", 300 * KH, ("scale_w", key), after + [("ld_w_" + wname,), ("ld_cols",)], emit)

        def through(name, wname, src, row, after):
            yield step("vector", 400, ("spread_bias", name), after,
                       lambda e: e.tensor_copy(spread_bias[:, :, :], src.unsqueeze(2).broadcast_to([P, KH, P])))
            slot, free = yield Take("work")

            def products(e):
                for k in range(KH):
                    last = e.matmul(work[slot][:, 0:H], spread_bias[:, k, :], w[wname][:, k, :],
                                    start=(k == 0), stop=(k == KH - 1))
                return last
            yield step("tensor", 900, ("through_mm", name), [("spread_bias", name), ("ld_w_" + wname,), free], products)
            r = rows[:, ROWS[row], :]
            yield step("vector", 350, ("through_add", name), [("through_mm", name), ("ld_rows",)],
                       lambda e: e.tensor_tensor(r, r, work[slot][:, 0:H], ALU.add))
            plan.free("work", slot, ("through_add", name))

        def folds():
            yield from fold("sq", "qkv", 0, 2, "ln1_b", 0, ("b_qkv", 0), L0_SCALE)
            yield from fold("skv", "qkv", 2, 4, "ln1_b", 2, ("b_qkv", 2), 1.0)
            yield scale_rows("sq", "qkv", 0, H, "ln1_s", L0_SCALE, [("fold_mm", "skv")])
            yield scale_rows("skv", "qkv", H, 3 * H, "ln1_s", 1.0, [("fold_mm", "skv")])
            yield step("vector", 150, ("add_self",), [("ld_mask_self",)],
                       lambda e: e.tensor_scalar(add_self[:, :], mask_self[:, :], 1.0, 10000.0, ALU.subtract, ALU.mult))
            yield from through("ao", "ao", folded[:, 4:6], "b_ao", [("fold_add", "skv")])
            yield from fold("cq", "q", 0, 2, "ln2_b", 6, ("b_q", 0), L0_SCALE)
            yield scale_rows("cq", "q", 0, H, "ln2_s", L0_SCALE, [("fold_mm", "cq")])
            yield from through("co", "co", col("b_kv", 2, 2), "b_co", [("through_mm", "ao")])
            yield from fold("m1", "m1", 0, 8, "ln3_b", 8, ("b1", 0), 1.0)
            yield scale_rows("m1", "m1", 0, FF, "ln3_s", 1.0, [("fold_mm", "m1")])
            yield scale_rows("lq", "lq", 0, H, None, L1_SCALE, [])
            yield step("vector", 100, ("scale_lqb",), [("ld_cols",)],
                       lambda e: e.tensor_scalar(col("q_b", 0, 2), col("q_b", 0, 2), L1_SCALE, None, ALU.mult))
            yield scale_rows("n1", "n1", 0, FF, "postnorm_w", 1.0, [])
            yield from through("lo", "lo", col("v_b", 0, 2), "out_b", [("through_mm", "co")])
            yield step("vector", 2300, ("mask_keys",), [("ld_mask_keys",)],
                       lambda e: e.tensor_scalar(mask_keys, mask_keys_i[:, :, :], 0, MASKED, ALU.is_equal, ALU.mult))

        def normed(u, tag, b, src, src_ready, eps, centred):
            k = lambda n: (n, u, tag)
            yield step("vector", 340, k("bn_stats"), src_ready, lambda e: e.bn_stats(b.bn[:, :], src))
            yield step("vector", 110, k("bn_aggr"), [k("bn_stats")], lambda e: e.bn_aggr(b.mv[:, :], b.bn[:, :]))
            if centred:
                yield step("vector", 70, k("var_eps"), [k("bn_aggr")],
                           lambda e: e.tensor_scalar(b.var[:, :], b.mv[:, 1:2], eps, None, ALU.add))
            else:
                yield step("vector", 70, k("mean_square"), [k("bn_aggr")],
                           lambda e: e.scalar_tensor_tensor(b.rs[:, 0:1], b.mv[:, 0:1], b.mv[:, 0:1], b.mv[:, 1:2],
                                                            ALU.mult, ALU.add))
                yield step("vector", 70, k("var_eps"), [k("mean_square")],
                           lambda e: e.tensor_scalar(b.var[:, :], b.rs[:, 0:1], eps, None, ALU.add))
            yield step("gpsimd", 600, k("rstd"), [k("var_eps"), ("minus_half",)],
                       lambda e: e.tensor_tensor(b.rstd[:, :], b.var[:, :], minus_half[:, :], ALU.pow))
            if centred:
                yield step("vector", 250, k("xn"), [k("rstd")],
                           lambda e: e.tensor_scalar(b.xn[:, :], src, b.mv[:, 0:1], b.rstd[:, 0:1],
                                                     ALU.subtract, ALU.mult))
            else:
                yield step("vector", 250, k("xn"), [k("rstd")],
                           lambda e: e.tensor_scalar(b.xn[:, :], src, b.rstd[:, 0:1], None, ALU.mult))
            yield from turned(u, tag, b, b.xn[:, :], [k("xn")])

        def turned(u, tag, b, src, src_ready):
            slot, free = yield Take("work")

            def turn(e):
                for h in range(KH):
                    last = e.transpose(work[slot][:, h * P:(h + 1) * P], src[:, h * P:(h + 1) * P], ident[:, :])
                return last
            yield step("tensor", 220, ("turn", u, tag), src_ready + [free, ("ident",)], turn)
            yield step("scalar", 300, ("xT", u, tag), [("turn", u, tag)],
                       lambda e: e.copy(b.xT[:, :, :], work[slot][:, 0:KH * P].rearrange("p (k t) -> p k t", k=KH)))
            plan.free("work", slot, ("xT", u, tag))

        def features(u, tag, parts, out_ap, bias, ready):
            slot, free = yield Take("work")
            n = sum(p[2] for p in parts)

            def products(e):
                f = 0
                for wt, c, tiles, xT in parts:
                    for i in range(tiles):
                        for k in range(KH):
                            last = e.matmul(work[slot][:, f * P:(f + 1) * P], wt[:, k, c + i * P:c + (i + 1) * P],
                                            xT[:, k, :], start=(k == 0), stop=(k == KH - 1))
                        f += 1
                return last
            yield step("tensor", 436 * n, ("feat_mm", u, tag), ready + [free], products)
            yield step("vector", 70 + 134 * n, ("feat", u, tag), [("feat_mm", u, tag)],
                       lambda e: e.tensor_tensor(out_ap, work[slot][:, 0:n * P].rearrange("p (f t) -> p f t", f=n),
                                                 bias.unsqueeze(2).broadcast_to([P, n, P]), ALU.add))
            plan.free("work", slot, ("feat", u, tag))

        def spread_keys(u, tag, kT, ready, box):
            slot, free = yield Take("spread")
            box.append(slot)
            first = [("spread0", slot)]
            yield dma((f"place_keys_{tag}{u % STREAMS}", u), ready + first + [free],
                      [(spread[slot][HD * h:HD * h + HD, :, h, :], kT[HD * h:HD * h + HD, :, :]) for h in range(HB)])

        def values(u, tag, b, i, wt, c, xT, ready):
            slot, free = yield Take("work")

            def products(e):
                for k in range(KH):
                    last = e.matmul(work[slot][:, 0:H], xT[:, k, :], wt[:, k, c:c + H], start=(k == 0), stop=(k == KH - 1))
                return last
            yield step("tensor", 864, ("val_mm", u, tag), ready + [free], products)
            v = work[slot][:, 0:H].rearrange("p (n e d) -> p n e d", n=NP, e=2)

            def place(e):
                for q in range(BU):
                    for odd in range(2):
                        c0 = odd * (HD + 1)
                        last = e.copy(b.val[i][S * odd:S * odd + S, q, :, c0:c0 + HD], v[S * q:S * q + S, :, odd, :])
                return last
            yield step("scalar", 640, ("val", u, tag), [("val_mm", u, tag), ("val1", u % STREAMS, i)], place)
            plan.free("work", slot, ("val", u, tag))

        def score(u, tag, b, spread_slot, q_ready):
            slot, free = yield Take("scores")

            def products(e):
                for h in range(KH):
                    for q in range(BU):
                        last = e.matmul(scores[slot][S * q:S * q + S, h * 512:(h + 1) * 512],
                                        b.qk[:, h, S * q:S * q + S],
                                        spread[spread_slot][:, h, :, S * q:S * q + S], start=True, stop=True)
                return last
            yield step("tensor", 1820, ("score", u, tag), q_ready + [(f"place_keys_{tag}{u % STREAMS}", u), free], products)
            plan.free("spread", spread_slot, ("score", u, tag))
            return slot

        def view(ap):
            return ap[:, :].rearrange("p (h k) -> p h k", h=NH)

        def over_heads(ap):
            return ap.unsqueeze(1).broadcast_to([P, NH, S])

        def over_keys(ap):
            return ap.unsqueeze(2).broadcast_to([P, NH, S])

        def mix(u, tag, b, n, ready):
            for c in range(2 * n):
                slot, free = yield Take("work")
                pr = b.prob[c // 2]
                src = pr[:, :, :].rearrange("p (n e) k -> p n (e k)", e=2)

                def turn(e, c=c, slot=slot, src=src):
                    for j in range(4):
                        last = e.transpose(work[slot][:, j * P:(j + 1) * P], src[:, (c % 2) * 4 + j, :], ident[:, :])
                    return last
                yield step("tensor", 440, ("prob_turn", u, tag, c), [ready[c // 2], free], turn)
                o = b.probT[:, 4 * c:4 * c + 4, :]
                i = work[slot][:, :].rearrange("p (n t) -> p n t", n=4)
                if c % 2:
                    key = ("probT_v", u, tag, c)
                    yield step("vector", 600, key, [("prob_turn", u, tag, c)], lambda e, o=o, i=i: e.tensor_copy(o, i))
                else:
                    key = ("probT_s", u, tag, c)
                    yield step("scalar", 480, key, [("prob_turn", u, tag, c)], lambda e, o=o, i=i: e.copy(o, i))
                plan.free("work", slot, key)
            slot, free = yield Take("mixed")

            def products(e):
                for q in range(BU):
                    for p in range(NP):
                        for i in range(n):
                            last = e.matmul(mixed[slot][S * q:S * q + S, p * VW:(p + 1) * VW],
                                            b.probT[:, i * NP + p, S * q:S * q + S], b.val[i][:, q, p, :],
                                            start=(i == 0), stop=(i == n - 1))
                return last
            yield step("tensor", 16 * n * 107, ("mix", u, tag),
                       [(("probT_v", "probT_s")[1 - c % 2], u, tag, c) for c in range(2 * n)]
                       + [("val", u, (tag, i)) for i in range(n)] + [free], products)
            m = mixed[slot][:, 0:NP * VW].rearrange("p (h d) -> p h d", d=HD + 1)
            yield step("vector", 100, ("denominator", u, tag), [("mix", u, tag)],
                       lambda e: e.reciprocal(b.rs[:, :].unsqueeze(2), m[:, :, HD:HD + 1]))
            yield step("vector", 340, ("heads", u, tag), [("denominator", u, tag)],
                       lambda e: e.tensor_tensor(b.xn[:, :].rearrange("p (h d) -> p h d", h=NH), m[:, :, 0:HD],
                                                 b.rs[:, :].unsqueeze(2).broadcast_to([P, NH, HD]), ALU.mult))
            plan.free("mixed", slot, ("heads", u, tag))
            yield from turned(u, (tag, "heads"), b, b.xn[:, :], [("heads", u, tag)])

        def projected(u, tag, lhs, wt, tiles, ready, add, out_ap):
            slot, free = yield Take("work")

            def products(e):
                for f in range(tiles):
                    last = e.matmul(work[slot][:, 0:H], lhs[:, f, :], wt[:, f, :], start=(f == 0), stop=(f == tiles - 1))
                return last
            yield step("tensor", 432 * tiles, ("proj_mm", u, tag), ready + [free], products)
            yield step("vector", 340, ("proj", u, tag), [("proj_mm", u, tag), ("plus_bias", u, tag)],
                       lambda e: e.tensor_tensor(out_ap, work[slot][:, 0:H], add, ALU.add))
            plan.free("work", slot, ("proj", u, tag))

        def plus_bias(u, tag, out_ap, in_ap, row, ready):
            return step("gpsimd", 700, ("plus_bias", u, tag), ready,
                        lambda e: e.tensor_tensor(out_ap, in_ap, rows[:, ROWS[row], :], ALU.add))

        def l0_attention(u, tag, b, sp, mask, add, mask_ready, q_ready):
            slot = yield from score(u, tag, b, sp, q_ready)
            pr = b.prob[0]
            yield step("vector", 1140, ("masked", u, tag), [("score", u, tag)] + mask_ready,
                       lambda e: e.tensor_tensor(pr[:, :, :], view(scores[slot]), over_heads(mask), ALU.mult))
            plan.free("scores", slot, ("masked", u, tag))
            yield step("gpsimd", 2400, ("masked2", u, tag), [("masked", u, tag)],
                       lambda e: e.tensor_tensor(pr[:, :, :], pr[:, :, :], over_heads(add), ALU.add))
            yield step("vector", 1140, ("max", u, tag), [("masked2", u, tag)],
                       lambda e: e.tensor_reduce(b.mx[0][:, :], pr[:, :, :], AX.X, ALU.max))
            yield step("vector", 1140, ("shifted", u, tag), [("max", u, tag)],
                       lambda e: e.tensor_tensor(pr[:, :, :], pr[:, :, :], over_keys(b.mx[0][:, :]), ALU.subtract))
            yield step("scalar", 960, ("exp", u, tag), [("shifted", u, tag)],
                       lambda e: e.activation(pr[:, :, :], pr[:, :, :], ACT.Exp))
            yield from mix(u, tag, b, 1, [("exp", u, tag)])

        def mlp(u, tag, b, w1, b1, w2, w_ready, add, out_ap):
            for g in range(2):
                slot, free = yield Take("work")

                def products(e, g=g, slot=slot):
                    for j in range(4):
                        for k in range(KH):
                            last = e.matmul(work[slot][:, j * P:(j + 1) * P], w1[:, k, (4 * g + j) * P:(4 * g + j + 1) * P],
                                            b.xT[:, k, :], start=(k == 0), stop=(k == KH - 1))
                    return last
                yield step("tensor", 1744, ("hid_mm", u, tag, g), [("xT", u, tag), free] + w_ready, products)

                def gelu(e, g=g, slot=slot):
                    for j in range(4):
                        last = e.activation(b.hid[:, 4 * g + j, :], work[slot][:, j * P:(j + 1) * P],
                                            ACT.Gelu_apprx_tanh, bias=b1[:, 4 * g + j:4 * g + j + 1])
                    return last
                yield step("scalar", 1000, ("hid", u, tag, g), [("hid_mm", u, tag, g)], gelu)
                plan.free("work", slot, ("hid", u, tag, g))
            yield from projected(u, tag, b.hid, w2, NF, [("hid", u, tag, 1)], add, out_ap)

        def unit(u, b):
            s = u % STREAMS
            before = [(f"store{s}", u - STREAMS)] if u >= STREAMS else []
            tok = slice(u * P, (u + 1) * P)
            yield dma((f"ld_unit{s}", u), before + ([("proj", u - STREAMS, "mlp1")] if u >= STREAMS else []),
                      [(b.x[:, :], x_in[tok, :]), (b.ctxT[:, :, :], ctxT_in[u]), (b.mask[:, :], mask_cross_in[tok, :])])
            loaded = (f"ld_unit{s}", u)

            yield plus_bias(u, "self", b.xb[:, :], b.x[:, :], "b_ao", [loaded, ("through_add", "ao")])
            yield from normed(u, "self", b, b.x[:, :], [loaded], L0_EPS, True)
            yield from features(u, "self", [(w["qkv"], 0, 4, b.xT)], b.qk[:, :, :], folded[:, 0:4],
                                [("xT", u, "self"), ("scale_w", "sq"), ("scale_w", "skv"), ("fold_add", "sq", 1), ("fold_add", "skv")])
            box = []
            yield from spread_keys(u, "self", b.qk[:, KH:, :], [("feat", u, "self")], box)
            yield from values(u, ("self", 0), b, 0, w["qkv"], 2 * H, b.xT, [])
            yield step("gpsimd", 250, ("add_cross", u), [loaded],
                       lambda e: e.tensor_scalar(b.add[:, :], b.mask[:, :], -1.0, 10000.0, ALU.add, ALU.mult))
            yield from l0_attention(u, "self", b, box[0], mask_self[:, :], add_self[:, :], [("add_self",)],
                                    [("feat", u, "self")])
            yield from projected(u, "self", b.xT, w["ao"], KH, [("xT", u, ("self", "heads")), ("ld_w_ao",)],
                                 b.xb[:, :], b.x[:, :])

            yield plus_bias(u, "cross", b.xb[:, :], b.x[:, :], "b_co", [("proj", u, "self"), ("through_add", "co")])
            yield from features(u, "cross_k", [(w["kv"], 0, 2, b.ctxT)], b.kc[:, :, :], col("b_kv", 0, 2),
                                [loaded, ("ld_w_kv",)])
            box = []
            yield from spread_keys(u, "cross", b.kc[:, :, :], [("feat", u, "cross_k")], box)
            yield from values(u, ("cross", 0), b, 0, w["kv"], H, b.ctxT, [])
            yield from normed(u, "cross", b, b.x[:, :], [("proj", u, "self")], L0_EPS, True)
            yield from features(u, "cross", [(w["q"], 0, 2, b.xT)], b.qk[:, 0:KH, :], folded[:, 6:8],
                                [("xT", u, "cross"), ("scale_w", "cq"), ("fold_add", "cq", 1)])
            yield from l0_attention(u, "cross", b, box[0], b.mask[:, :], b.add[:, :], [("add_cross", u)],
                                    [("feat", u, "cross")])
            yield from projected(u, "cross", b.xT, w["co"], KH, [("xT", u, ("cross", "heads")), ("ld_w_co",)],
                                 b.xb[:, :], b.x[:, :])

            yield plus_bias(u, "mlp0", b.xb[:, :], b.x[:, :], "b2", [("proj", u, "cross")])
            yield from normed(u, "mlp0", b, b.x[:, :], [("proj", u, "cross")], L0_EPS, True)
            yield from mlp(u, "mlp0", b, w["m1"], folded[:, 8:16], w["m2"],
                           [("scale_w", "m1"), ("fold_add", "m1"), ("ld_w_m2",)], b.xb[:, :], b.x[:, :])

            yield plus_bias(u, "lat", b.xb[:, :], b.x[:, :], "out_b", [("proj", u, "mlp0"), ("through_add", "lo")])
            yield from features(u, "ctx_k", [(w["lk"], 0, 2, b.ctxT)], b.kc[:, :, :], col("k_b", 0, 2), [("ld_w_lk",)])
            box = []
            yield from spread_keys(u, "ctx", b.kc[:, :, :], [("feat", u, "ctx_k")], box)
            yield from values(u, ("lat", 0), b, 0, w["lv"], 0, b.ctxT, [("ld_w_lv",)])
            yield from turned(u, "lat", b, b.x[:, :], [("proj", u, "mlp0")])
            yield from features(u, "lat_q", [(w["lq"], 0, 2, b.xT)], b.qk[:, 0:KH, :], col("q_b", 0, 2),
                                [("xT", u, "lat"), ("scale_w", "lq"), ("scale_lqb",)])
            yield from features(u, "lat_k", [(w["lk"], 0, 2, b.xT)], b.qk[:, KH:, :], col("k_b", 0, 2), [])
            slot_c = yield from score(u, "ctx", b, box[0], [("feat", u, "lat_q")])
            pc, pl = b.prob
            yield step("vector", 1140, ("masked", u, "ctx"), [("score", u, "ctx"), ("mask_keys",)],
                       lambda e: e.tensor_tensor(pc[:, :, :], view(scores[slot_c]), over_heads(mask_keys[:, u, :]), ALU.add))
            plan.free("scores", slot_c, ("masked", u, "ctx"))
            box = []
            yield from spread_keys(u, "lat", b.qk[:, KH:, :], [("feat", u, "lat_k")], box)
            yield from values(u, ("lat", 1), b, 1, w["lv"], 0, b.xT, [])
            yield step("vector", 1140, ("max", u, "ctx"), [("masked", u, "ctx")],
                       lambda e: e.tensor_reduce(b.mx[0][:, :], pc[:, :, :], AX.X, ALU.max))
            slot_l = yield from score(u, "lat", b, box[0], [("feat", u, "lat_q")])
            yield step("vector", 1140, ("max", u, "lat"), [("score", u, "lat")],
                       lambda e: e.tensor_reduce(b.mx[1][:, :], view(scores[slot_l]), AX.X, ALU.max))
            yield step("vector", 80, ("max", u, "both"), [("max", u, "lat"), ("max", u, "ctx")],
                       lambda e: e.tensor_tensor(b.mx[0][:, :], b.mx[0][:, :], b.mx[1][:, :], ALU.max))
            yield step("vector", 1140, ("shifted", u, "lat"), [("max", u, "both")],
                       lambda e: e.tensor_tensor(pl[:, :, :], view(scores[slot_l]), over_keys(b.mx[0][:, :]), ALU.subtract))
            plan.free("scores", slot_l, ("shifted", u, "lat"))
            yield step("gpsimd", 2400, ("shifted2", u, "ctx"), [("max", u, "both")],
                       lambda e: e.tensor_tensor(pc[:, :, :], pc[:, :, :], over_keys(b.mx[0][:, :]), ALU.subtract))
            yield step("scalar", 960, ("exp", u, "lat"), [("shifted", u, "lat")],
                       lambda e: e.activation(pl[:, :, :], pl[:, :, :], ACT.Exp))
            yield step("scalar", 960, ("exp", u, "ctx"), [("shifted2", u, "ctx")],
                       lambda e: e.activation(pc[:, :, :], pc[:, :, :], ACT.Exp))
            yield from mix(u, "lat", b, 2, [("exp", u, "ctx"), ("exp", u, "lat")])
            yield from projected(u, "lat", b.xT, w["lo"], KH, [("xT", u, ("lat", "heads")), ("ld_w_lo",)],
                                 b.xb[:, :], b.xb[:, :])

            yield plus_bias(u, "mlp1", b.x[:, :], b.x[:, :], "mlp_b2", [("plus_bias", u, "lat"), ("turn", u, "lat")])
            yield from normed(u, "mlp1", b, b.xb[:, :], [("proj", u, "lat")], L1_EPS, False)
            yield from mlp(u, "mlp1", b, w["n1"], col("mlp_b1", 0, 8), w["n2"],
                           [("scale_w", "n1"), ("ld_w_n2",)], b.x[:, :], b.xb[:, :])
            yield dma((f"store{s}", u), [("proj", u, "mlp1")], [(out[tok, :], b.xb[:, :])])

        def stream(s):
            for u in range(s, UNITS, STREAMS):
                yield from unit(u, bufs[s])

        plan.weave([constants(), setup(), folds()] + [stream(s) for s in range(STREAMS)])

        block = ctx.enter_context(nc.Block())

        @block.tensor
        def _(eng):
            for run in plan.queues["tensor"]:
                run(eng)

        @block.vector
        def _(eng):
            for run in plan.queues["vector"]:
                run(eng)

        @block.scalar
        def _(eng):
            for run in plan.queues["scalar"]:
                run(eng)

        @block.gpsimd
        def _(eng):
            for run in plan.queues["gpsimd"]:
                run(eng)

        @block.sync
        def _(eng):
            for run in plan.queues["sync"]:
                run(eng)
            for s in range(STREAMS):
                eng.wait_ge(plan.sems[f"store{s}"], plan.count[f"store{s}"])


def kernel(**inputs):
    import concourse.bacc as bacc
    from concourse.bass_utils import run_bass_kernel_spmd as launch

    a = {k: np.ascontiguousarray(v) for k, v in inputs.items()}
    l0 = lambda n: a["L0_xattn_" + n]
    l1 = lambda n: a["L1_xattn_" + n]

    def columns(v):
        return v.reshape(-1, P).T

    kv_w = l1("kv_w").reshape(H, H, 2)
    kv_b = l1("kv_b").reshape(H, 2)
    cols = {"ln1_s": l0("ln1_s"), "ln1_b": l0("ln1_b"), "b_qkv": l0("b_qkv"), "ln2_s": l0("ln2_s"),
            "ln2_b": l0("ln2_b"), "b_q": l0("b_q"), "b_kv": l0("b_kv"), "ln3_s": l0("ln3_s"),
            "ln3_b": l0("ln3_b"), "b1": l0("b1"), "q_b": l1("q_b"), "k_b": kv_b[:, 0], "v_b": kv_b[:, 1],
            "postnorm_w": l1("postnorm_w"), "mlp_b1": l1("mlp_b1")}
    rows = {"b_ao": l0("b_ao"), "b_co": l0("b_co"), "b2": l0("b2"), "out_b": l1("out_b"), "mlp_b2": l1("mlp_b2")}
    weights = {"qkv": l0("w_qkv"), "ao": l0("w_ao"), "q": l0("w_q"), "kv": l0("w_kv"), "co": l0("w_co"),
               "m1": l0("w1"), "m2": l0("w2"), "lq": l1("q_w"), "lk": kv_w[:, :, 0], "lv": kv_w[:, :, 1],
               "lo": l1("out_w"), "n1": l1("mlp_w1"), "n2": l1("mlp_w2")}
    arrays = {
        "x": a["x"].reshape(B * S, H),
        "ctxT": a["ctx_2048"].reshape(UNITS, P, KH, P).transpose(0, 3, 2, 1),
        "mask_self": a["mask_1x1xSxS2_fc1"].reshape(S, S),
        "mask_cross": a["mask_Bx1xSxS2_ff1"].reshape(B * S, S),
        "mask_keys": a["mask_BxS2_ik0"],
        "cols": np.concatenate([columns(cols[n]) for n in COLS], axis=1),
        "rows": np.stack([rows[n] for n in ROWS])[None],
    }
    arrays.update({"w_" + n: v for n, v in weights.items()})
    arrays = {k: np.ascontiguousarray(v) for k, v in arrays.items()}

    nc = bacc.Bacc("TRN2", target_bir_lowering=False, num_devices=1)
    d = {k: nc.dram_tensor("in_" + k, v.shape, mybir.dt.from_np(v.dtype), kind="ExternalInput").ap()
         for k, v in arrays.items()}
    out = nc.dram_tensor("out", (B * S, H), F32, kind="ExternalOutput").ap()
    build(nc, d["x"], d["ctxT"], d["mask_self"], d["mask_cross"], d["mask_keys"], d["cols"], d["rows"],
          {n: d["w_" + n] for n in weights}, out)
    r = launch(nc, [{"in_" + k: v for k, v in arrays.items()}], core_ids=[0])
    return r.results[0]["out"].reshape(B, S, H)
```

```python
from contextlib import ExitStack

import numpy as np

import concourse.bass as bass
from concourse import mybir

F32 = mybir.dt.float32
I32 = mybir.dt.int32
ALU = mybir.AluOpType
ACT = mybir.ActivationFunctionType
AX = mybir.AxisListType

P = 128
B, S, H = 64, 64, 256
NH = 16
HD = H // NH
KH = H // P
HB = P // HD
NP = NH // 2
FF = 4 * H
NF = FF // P
BU = P // S
UNITS = B // BU
STREAMS = 4
HH = NH // 2
SCORE_BANKS, MIXED_BANKS = 2, 1
OWN_KEYS, CTX_KEYS = 2, 2
CHUNKS, TURNED_CHUNKS = 11, 6
VW = 2 * (HD + 1)
L0_EPS, L1_EPS = 1e-5, 1e-6
L0_SCALE = float(HD) ** -0.5
L1_SCALE = 1.0 / HD

SEEN = {"tensor": 350, "vector": 300, "scalar": 300, "gpsimd": 300}
DMA_HOLD, DMA_SEEN = 600, 2500
TABLES = ("exp", "hid")
TABLE_NS = 1000
AGE = 70
TIE = 50

MASKED = -1e30

COLS = {}
for _name, _n in (("ln1_s", 2), ("ln1_b", 2), ("b_qkv", 6), ("ln2_s", 2), ("ln2_b", 2), ("b_q", 2),
                  ("b_kv", 4), ("ln3_s", 2), ("ln3_b", 2), ("b1", 8), ("q_b", 2), ("k_b", 2),
                  ("v_b", 2), ("postnorm_w", 2), ("mlp_b1", 8)):
    COLS[_name] = (sum(n for _, n in COLS.values()), _n)
NCOLS = sum(n for _, n in COLS.values())
ROWS = {n: i for i, n in enumerate(("b_ao", "b_co", "b2", "out_b", "mlp_b2"))}


class Step:

    def __init__(self, engine, ns, name, after, emit, dmas=0):
        self.engine, self.ns, self.name, self.emit, self.dmas = engine, ns, name, emit, dmas
        self.table = name[0] if name[0] in TABLES else None
        self.unit = name[1] if len(name) > 1 and isinstance(name[1], int) else 0
        self.after = [k for k in after if k is not None]


class Take:
    def __init__(self, pool):
        self.pool = pool


class Behind:

    def __init__(self, key):
        self.key = key


class Plan:

    def __init__(self, nc, ctx):
        self.nc, self.ctx = nc, ctx
        self.queues = {e: [] for e in ("sync", "gpsimd", "scalar", "vector", "tensor")}
        self.sems, self.count, self.value, self.owner = {}, {}, {}, {}
        self.waited = {e: {} for e in self.queues}
        self.engine_free = {e: 0.0 for e in self.queues}
        self.at = {}
        self.table = None
        self.pools = {}

    def add(self, step):
        kind = step.name[0]
        assert self.owner.setdefault(kind, step.engine) == step.engine, kind
        if kind not in self.sems:
            self.sems[kind] = self.ctx.enter_context(self.nc.semaphore("s_" + kind))
            self.count[kind] = 0
        waits = []
        for key in step.after:
            v = self.value[key]
            if self.waited[step.engine].get(key[0], 0) < v:
                self.waited[step.engine][key[0]] = v
                waits.append((self.sems[key[0]], v))
        dmas = step.dmas
        self.count[kind] += 16 * dmas if dmas else 1
        self.value[step.name] = self.count[kind]
        sem = self.sems[kind]

        def run(eng):
            for s, v in waits:
                eng.wait_ge(s, v)
            last = step.emit(eng)
            if dmas:
                assert len(last) == dmas
                for i in last:
                    i.then_inc(sem, 16)
            else:
                last.then_inc(sem, 1)
        self.queues[step.engine].append(run)
        start = self.start(step)
        if step.table:
            self.table = step.table
        self.engine_free[step.engine] = start + (DMA_HOLD * dmas or step.ns)
        self.at[step.name] = start + step.ns + (DMA_SEEN + DMA_HOLD * dmas if dmas else SEEN[step.engine])

    def start(self, step):
        ready = max([self.engine_free[step.engine]] + [self.at[k] for k in step.after])
        return ready + (TABLE_NS if step.table and step.table != self.table else 0)

    def known(self, step):
        return all(k in self.value for k in step.after)

    def pool(self, name, slots):
        self.pools[name] = [(i, None) for i in range(slots)]

    def free(self, name, slot, key):
        self.pools[name].append((slot, key))

    def weave(self, streams):
        heads = [(next(s), s) for s in streams]
        while heads:
            best = None
            for n, (head, s) in enumerate(heads):
                while True:
                    if isinstance(head, Take) and self.pools[head.pool]:
                        head = s.send(self.pools[head.pool].pop(0))
                    elif isinstance(head, Behind) and head.key in self.value:
                        head = next(s)
                    else:
                        break
                    heads[n] = (head, s)
                if not isinstance(head, Step) or not self.known(head):
                    continue
                t = self.start(head)
                t += AGE * head.unit
                if best is None or t < best[0] - TIE:
                    best = (t, n)
            assert best is not None, [h.pool if isinstance(h, Take) else h.key if isinstance(h, Behind) else (h.name, h.after) for h, _ in heads]
            head, s = heads[best[1]]
            self.add(head)
            try:
                heads[best[1]] = (next(s), s)
            except StopIteration:
                del heads[best[1]]


def build(nc, x_in, ctxT_in, mask_self_in, mask_cross_in, mask_keys_in, cols_in, rows_in, weights_in,
          out):
    with ExitStack() as ctx:
        def sb(name, shape, dt=F32):
            return ctx.enter_context(nc.sbuf_tensor(name, shape, dt))

        plan = Plan(nc, ctx)

        def banks(name, n):
            plan.pool(name, n)
            return [ctx.enter_context(nc.psum_tensor(f"{name}{i}", [P, 512], F32)) for i in range(n)]

        scores = banks("scores", SCORE_BANKS)
        mixed = banks("mixed", MIXED_BANKS)
        work = banks("work", 8 - SCORE_BANKS - MIXED_BANKS)

        w = {name: sb("w_" + name, [P, ap.shape[0] // P, ap.shape[1]]) for name, ap in weights_in.items()}
        cols = sb("cols", [P, NCOLS])
        rows = sb("rows", [P, len(ROWS), H])
        folded = sb("folded", [P, 16])
        spread_bias = sb("spread_bias", [P, KH, P])
        ident = sb("ident", [P, P])
        minus_half = sb("minus_half", [P, 1])
        mask_self = sb("mask_self", [P, S])
        add_self = sb("add_self", [P, S])
        mask_keys_i = sb("mask_keys_i", [P, UNITS, S], I32)
        mask_keys = mask_keys_i[:, :, :].bitcast(F32)

        spread = [sb(f"spread{i}", [P, KH, HB, P]) for i in range(OWN_KEYS + CTX_KEYS)]
        plan.pools["own_keys"] = [(i, None) for i in range(OWN_KEYS)]
        plan.pools["ctx_keys"] = [(OWN_KEYS + i, None) for i in range(CTX_KEYS)]

        chunk = [sb(f"chunk{i}", [P, 512]) for i in range(CHUNKS)]
        plan.pool("chunk", CHUNKS)
        turned_chunk = [sb(f"turned_chunk{i}", [P, 4, P]) for i in range(TURNED_CHUNKS)]
        plan.pool("turned_chunk", TURNED_CHUNKS)

        spread_at = {}

        class Buffers:
            pass

        bufs = []
        for s in range(STREAMS):
            b = Buffers()
            b.xin = sb(f"xin{s}", [P, H])
            b.x = sb(f"x{s}", [P, H])
            b.xb = sb(f"xb{s}", [P, H])
            b.xn = sb(f"xn{s}", [P, H])
            b.xT = sb(f"xT{s}", [P, KH, P])
            b.ctxT = sb(f"ctxT{s}", [P, KH, P])
            b.qk = sb(f"qk{s}", [P, 2 * KH, P])
            b.kc = sb(f"kc{s}", [P, KH, P])
            b.val = [sb(f"val{s}_{i}", [P, BU, NP, VW]) for i in range(2)]
            b.mask = sb(f"mask{s}", [P, S])
            b.add = sb(f"add{s}", [P, S])
            b.bn = sb(f"bn{s}", [P, 6])
            b.mv = sb(f"mv{s}", [P, 2])
            b.var = sb(f"var{s}", [P, 1])
            b.rstd = sb(f"rstd{s}", [P, 1])
            b.mx = [sb(f"mx{s}_{i}", [P, NH]) for i in range(2)]
            b.rs = sb(f"rs{s}", [P, NH])
            bufs.append(b)

        def col(name, i=0, n=1):
            c = COLS[name][0] + i
            return cols[:, c:c + n]

        def step(engine, ns, name, after, emit):
            return Step(engine, ns, name, after, emit)

        def dma(name, after, pairs):
            return Step("sync", 0, name, after, lambda eng: [eng.dma_start(o, i) for o, i in pairs],
                        dmas=len(pairs))

        def setup():
            yield dma(("ld_cols",), [], [(cols[:, :], cols_in)])
            yield dma(("ld_w_qkv",), [], [(w["qkv"][:, :, :], weights_in["qkv"].rearrange("(k p) n -> p k n", p=P))])
            for name in ("ao", "q", "kv", "co", "m1", "m2", "lq", "lk", "lv", "lo", "n1", "n2"):
                if name == "q":
                    yield dma(("ld_rows",), [], [(rows[:, :, :], rows_in.broadcast_to([P, len(ROWS), H]))])
                    yield dma(("ld_mask_self",), [], [(mask_self[S * b:S * b + S, :], mask_self_in) for b in range(BU)])
                yield dma((f"ld_w_{name}",), [], [(w[name][:, :, :], weights_in[name].rearrange("(k p) n -> p k n", p=P))])
            yield dma(("ld_mask_keys",), [],
                      [(mask_keys_i[S * b:S * b + S, :, :],
                        mask_keys_in.rearrange("(u b) k -> b u k", b=BU)[b:b + 1].broadcast_to([S, UNITS, S]))
                       for b in range(BU)])

        def constants():
            yield step("gpsimd", 200, ("ident0",), [], lambda e: e.memset(ident[:, :], 0.0))
            yield step("gpsimd", 200, ("ident",), [("ident0",)],
                       lambda e: e.affine_select(out=ident[:, :], in_=ident[:, :], compare_op=ALU.not_equal,
                                                 fill=1.0, base=0, pattern=[[-1, P]], channel_multiplier=1))
            yield step("gpsimd", 100, ("minus_half",), [], lambda e: e.memset(minus_half[:, :], -0.5))
            for s in range(STREAMS):
                for i in range(2):
                    v = bufs[s].val[i]
                    yield step("vector", 600, ("val0", s, i), [], lambda e, v=v: e.memset(v[:, :, :, :], 0.0))

                    def ones(e, v=v):
                        for half in range(2):
                            last = e.memset(v[S * half:S * half + S, :, :, half * (HD + 1) + HD:half * (HD + 1) + HD + 1], 1.0)
                        return last
                    yield step("vector", 200, ("val1", s, i), [("val0", s, i)], ones)
            for i in range(OWN_KEYS + CTX_KEYS):
                yield step("gpsimd", 2200, ("spread0", i), [], lambda e, i=i: e.memset(spread[i][:, :, :, :], 0.0))

        def fold(name, wname, first, tiles, beta, at, bias, scale):
            slot, free = yield Take("work")

            def products(e):
                for f in range(tiles):
                    for k in range(KH):
                        last = e.matmul(work[slot][:, f:f + 1], w[wname][:, k, (first + f) * P:(first + f + 1) * P],
                                        col(beta, k), start=(k == 0), stop=(k == KH - 1))
                return last
            yield step("tensor", 900 * tiles, ("fold_mm", name), [("ld_w_" + wname,), ("ld_cols",), free], products)
            yield step("vector", 100, ("fold_add", name), [("fold_mm", name)],
                       lambda e: e.tensor_tensor(folded[:, at:at + tiles], work[slot][:, 0:tiles],
                                                 col(bias[0], bias[1], tiles), ALU.add))
            plan.free("work", slot, ("fold_add", name))
            if scale != 1.0:
                yield step("vector", 100, ("fold_add", name, 1), [("fold_add", name)],
                           lambda e: e.tensor_scalar(folded[:, at:at + tiles], folded[:, at:at + tiles],
                                                     scale, None, ALU.mult))

        def scale_rows(key, wname, lo, hi, s_col, scale, after):
            def emit(e):
                for k in range(KH):
                    a = w[wname][:, k, lo:hi]
                    if s_col is None:
                        last = e.tensor_scalar(a, a, scale, None, ALU.mult)
                    else:
                        last = e.tensor_scalar(a, a, col(s_col, k), scale, ALU.mult, ALU.mult)
                return last
            return step("vector", 300 * KH, ("scale_w", key), after + [("ld_w_" + wname,), ("ld_cols",)], emit)

        def through(name, wname, src, row, after):
            yield step("vector", 400, ("spread_bias", name), after,
                       lambda e: e.tensor_copy(spread_bias[:, :, :], src.unsqueeze(2).broadcast_to([P, KH, P])))
            slot, free = yield Take("work")

            def products(e):
                for k in range(KH):
                    last = e.matmul(work[slot][:, 0:H], spread_bias[:, k, :], w[wname][:, k, :],
                                    start=(k == 0), stop=(k == KH - 1))
                return last
            yield step("tensor", 900, ("through_mm", name), [("spread_bias", name), ("ld_w_" + wname,), free], products)
            r = rows[:, ROWS[row], :]
            yield step("vector", 350, ("through_add", name), [("through_mm", name), ("ld_rows",)],
                       lambda e: e.tensor_tensor(r, r, work[slot][:, 0:H], ALU.add))
            plan.free("work", slot, ("through_add", name))

        def folds():
            yield from fold("sq", "qkv", 0, 2, "ln1_b", 0, ("b_qkv", 0), L0_SCALE)
            yield from fold("skv", "qkv", 2, 4, "ln1_b", 2, ("b_qkv", 2), 1.0)
            yield scale_rows("sq", "qkv", 0, H, "ln1_s", L0_SCALE, [("fold_mm", "skv")])
            yield scale_rows("skv", "qkv", H, 3 * H, "ln1_s", 1.0, [("fold_mm", "skv")])
            yield step("vector", 150, ("add_self",), [("ld_mask_self",)],
                       lambda e: e.tensor_scalar(add_self[:, :], mask_self[:, :], 1.0, 10000.0, ALU.subtract, ALU.mult))
            yield from through("ao", "ao", folded[:, 4:6], "b_ao", [("fold_add", "skv")])
            yield from fold("cq", "q", 0, 2, "ln2_b", 6, ("b_q", 0), L0_SCALE)
            yield scale_rows("cq", "q", 0, H, "ln2_s", L0_SCALE, [("fold_mm", "cq")])
            yield from through("co", "co", col("b_kv", 2, 2), "b_co", [("through_mm", "ao")])
            yield from fold("m1", "m1", 0, 8, "ln3_b", 8, ("b1", 0), 1.0)
            yield scale_rows("m1", "m1", 0, FF, "ln3_s", 1.0, [("fold_mm", "m1")])
            yield scale_rows("lq", "lq", 0, H, None, L1_SCALE, [])
            yield step("vector", 100, ("scale_lqb",), [("ld_cols",)],
                       lambda e: e.tensor_scalar(col("q_b", 0, 2), col("q_b", 0, 2), L1_SCALE, None, ALU.mult))
            yield scale_rows("n1", "n1", 0, FF, "postnorm_w", 1.0, [])
            yield from through("lo", "lo", col("v_b", 0, 2), "out_b", [("through_mm", "co")])
            yield step("vector", 2300, ("mask_keys",), [("ld_mask_keys",)],
                       lambda e: e.tensor_scalar(mask_keys, mask_keys_i[:, :, :], 0, MASKED, ALU.is_equal, ALU.mult))

        def normed(u, tag, b, src, src_ready, eps, centred):
            k = lambda n: (n, u, tag)
            yield step("vector", 340, k("bn_stats"), src_ready, lambda e: e.bn_stats(b.bn[:, :], src))
            yield step("vector", 110, k("bn_aggr"), [k("bn_stats")], lambda e: e.bn_aggr(b.mv[:, :], b.bn[:, :]))
            if centred:
                yield step("vector", 70, k("var_eps"), [k("bn_aggr")],
                           lambda e: e.tensor_scalar(b.var[:, :], b.mv[:, 1:2], eps, None, ALU.add))
            else:
                yield step("vector", 70, k("mean_square"), [k("bn_aggr")],
                           lambda e: e.scalar_tensor_tensor(b.rs[:, 0:1], b.mv[:, 0:1], b.mv[:, 0:1], b.mv[:, 1:2],
                                                            ALU.mult, ALU.add))
                yield step("vector", 70, k("var_eps"), [k("mean_square")],
                           lambda e: e.tensor_scalar(b.var[:, :], b.rs[:, 0:1], eps, None, ALU.add))
            yield step("gpsimd", 600, k("rstd"), [k("var_eps"), ("minus_half",)],
                       lambda e: e.tensor_tensor(b.rstd[:, :], b.var[:, :], minus_half[:, :], ALU.pow))
            if centred:
                yield step("vector", 250, k("xn"), [k("rstd")],
                           lambda e: e.tensor_scalar(b.xn[:, :], src, b.mv[:, 0:1], b.rstd[:, 0:1],
                                                     ALU.subtract, ALU.mult))
            else:
                yield step("vector", 250, k("xn"), [k("rstd")],
                           lambda e: e.tensor_scalar(b.xn[:, :], src, b.rstd[:, 0:1], None, ALU.mult))
            yield from turned(u, tag, b, b.xn[:, :], [k("xn")])

        def turned(u, tag, b, src, src_ready):
            slot, free = yield Take("work")

            def turn(e):
                for h in range(KH):
                    last = e.transpose(work[slot][:, h * P:(h + 1) * P], src[:, h * P:(h + 1) * P], ident[:, :])
                return last
            yield step("tensor", 220, ("turn", u, tag), src_ready + [free, ("ident",)], turn)
            yield step("scalar", 300, ("xT", u, tag), [("turn", u, tag)],
                       lambda e: e.copy(b.xT[:, :, :], work[slot][:, 0:KH * P].rearrange("p (k t) -> p k t", k=KH)))
            plan.free("work", slot, ("xT", u, tag))

        def features(u, tag, parts, out_ap, bias, ready):
            slot, free = yield Take("work")
            n = sum(p[2] for p in parts)

            def products(e):
                f = 0
                for wt, c, tiles, xT in parts:
                    for i in range(tiles):
                        for k in range(KH):
                            last = e.matmul(work[slot][:, f * P:(f + 1) * P], wt[:, k, c + i * P:c + (i + 1) * P],
                                            xT[:, k, :], start=(k == 0), stop=(k == KH - 1))
                        f += 1
                return last
            yield step("tensor", 436 * n, ("feat_mm", u, tag), ready + [free], products)
            yield step("vector", 70 + 134 * n, ("feat", u, tag), [("feat_mm", u, tag)],
                       lambda e: e.tensor_tensor(out_ap, work[slot][:, 0:n * P].rearrange("p (f t) -> p f t", f=n),
                                                 bias.unsqueeze(2).broadcast_to([P, n, P]), ALU.add))
            plan.free("work", slot, ("feat", u, tag))

        def spread_keys(u, tag, kT, ready, pool):
            slot, free = yield Take(pool)
            spread_at[u, tag] = pool, slot
            first = [("spread0", slot)]
            yield dma((f"place_keys_{tag}{u % STREAMS}", u), ready + first + [free],
                      [(spread[slot][HD * h:HD * h + HD, :, h, :], kT[HD * h:HD * h + HD, :, :]) for h in range(HB)])

        def values(u, tag, b, i, wt, c, xT, ready):
            slot, free = yield Take("work")

            def products(e):
                for k in range(KH):
                    last = e.matmul(work[slot][:, 0:H], xT[:, k, :], wt[:, k, c:c + H], start=(k == 0), stop=(k == KH - 1))
                return last
            yield step("tensor", 864, ("val_mm", u, tag), ready + [free], products)
            v = work[slot][:, 0:H].rearrange("p (n e d) -> p n e d", n=NP, e=2)

            def place(e):
                for q in range(BU):
                    for odd in range(2):
                        c0 = odd * (HD + 1)
                        last = e.copy(b.val[i][S * odd:S * odd + S, q, :, c0:c0 + HD], v[S * q:S * q + S, :, odd, :])
                return last
            yield step("scalar", 640, ("val", u, tag), [("val_mm", u, tag), ("val1", u % STREAMS, i)], place)
            plan.free("work", slot, ("val", u, tag))

        def score(u, tag, h, b, q_ready):
            yield Behind((f"place_keys_{tag}{u % STREAMS}", u))
            pool, sp = spread_at[u, tag]
            slot, free = yield Take("scores")

            def products(e):
                for q in range(BU):
                    last = e.matmul(scores[slot][S * q:S * q + S, :], b.qk[:, h, S * q:S * q + S],
                                    spread[sp][:, h, :, S * q:S * q + S], start=True, stop=True)
                return last
            yield step("tensor", 910, ("score", u, tag, h),
                       q_ready + [(f"place_keys_{tag}{u % STREAMS}", u), free], products)
            if h == KH - 1:
                plan.free(pool, sp, ("score", u, tag, h))
            return slot

        def by_key(ap):
            return ap.rearrange("p (h k) -> p h k", h=HH)

        def over_heads(ap):
            return ap.unsqueeze(1).broadcast_to([P, HH, S])

        def over_keys(ap):
            return ap.unsqueeze(2).broadcast_to([P, HH, S])

        def max_of(b, i, h):
            return b.mx[i][:, HH * h:HH * h + HH]

        def turn_chunk(u, tag, i, h, b, c, ready):
            slot, free = yield Take("work")

            def turn(e):
                for j in range(4):
                    last = e.transpose(work[slot][:, j * P:(j + 1) * P], chunk[c][:, j * P:(j + 1) * P], ident[:, :])
                return last
            yield step("tensor", 440, ("prob_turn", u, tag, i, h), [ready, free], turn)
            plan.free("chunk", c, ("prob_turn", u, tag, i, h))
            t, t_free = yield Take("turned_chunk")
            src = work[slot][:, :].rearrange("p (n t) -> p n t", n=4)
            key = ("probT", u, tag, i, h)
            yield step("scalar", 480, key, [("prob_turn", u, tag, i, h), t_free],
                       lambda e: e.copy(turned_chunk[t][:, :, :], src))
            plan.free("work", slot, key)
            return t

        def mix_half(u, tag, h, b, slot, free, turned_at):
            def products(e):
                for q in range(BU):
                    for j in range(NP // 2):
                        p = h * (NP // 2) + j
                        for n, (i, t) in enumerate(turned_at):
                            last = e.matmul(mixed[slot][S * q:S * q + S, p * VW:(p + 1) * VW],
                                            turned_chunk[t][:, j, S * q:S * q + S], b.val[i][:, q, p, :],
                                            start=(n == 0), stop=(n == len(turned_at) - 1))
                return last
            yield step("tensor", 8 * len(turned_at) * 107, ("mix", u, tag, h),
                       [("probT", u, tag, i, h) for i, _ in turned_at]
                       + [("val", u, (tag, i)) for i, _ in turned_at] + [free], products)
            for _, t in turned_at:
                plan.free("turned_chunk", t, ("mix", u, tag, h))

        def divided(u, tag, b, slot):
            m = mixed[slot][:, 0:NP * VW].rearrange("p (h d) -> p h d", d=HD + 1)
            yield step("vector", 100, ("denominator", u, tag), [("mix", u, tag, 1)],
                       lambda e: e.reciprocal(b.rs[:, :].unsqueeze(2), m[:, :, HD:HD + 1]))
            yield step("vector", 340, ("heads", u, tag), [("denominator", u, tag)],
                       lambda e: e.tensor_tensor(b.xn[:, :].rearrange("p (h d) -> p h d", h=NH), m[:, :, 0:HD],
                                                 b.rs[:, :].unsqueeze(2).broadcast_to([P, NH, HD]), ALU.mult))
            plan.free("mixed", slot, ("heads", u, tag))
            yield from turned(u, (tag, "heads"), b, b.xn[:, :], [("heads", u, tag)])

        def projected(u, tag, tiles, ready, add, out_ap):
            slot, free = yield Take("work")
            for part in sorted(ready):
                mine = [n for n, t in enumerate(tiles) if t[0] == part]

                def products(e, mine=mine):
                    for n in mine:
                        last = e.matmul(work[slot][:, 0:H], tiles[n][1], tiles[n][2], start=(n == 0), stop=(n == len(tiles) - 1))
                    return last
                yield step("tensor", 432 * len(mine), ("proj_mm", u, tag, part), ready[part] + [free], products)
            yield step("vector", 340, ("proj", u, tag), [("proj_mm", u, tag, max(ready)), ("plus_bias", u, tag)],
                       lambda e: e.tensor_tensor(out_ap, work[slot][:, 0:H], add, ALU.add))
            plan.free("work", slot, ("proj", u, tag))

        def plus_bias(u, tag, out_ap, in_ap, row, ready):
            return step("gpsimd", 700, ("plus_bias", u, tag), ready,
                        lambda e: e.tensor_tensor(out_ap, in_ap, rows[:, ROWS[row], :], ALU.add))

        def l0_attention(u, tag, v, b, mask, add, mask_ready, q_ready):
            at, c = [None] * 2, [None] * 2
            for h in range(2):
                at[h] = yield from score(u, tag, h, b, q_ready)
                c[h], free = yield Take("chunk")
                ch, ps = by_key(chunk[c[h]][:, :]), by_key(scores[at[h]][:, :])
                yield step("vector", 600, ("masked", u, tag, h), [("score", u, tag, h), free] + mask_ready,
                           lambda e, ch=ch, ps=ps: e.tensor_tensor(ch, ps, over_heads(mask), ALU.mult))
                plan.free("scores", at[h], ("masked", u, tag, h))
                yield step("gpsimd", 1250, ("masked2", u, tag, h), [("masked", u, tag, h)],
                           lambda e, ch=ch: e.tensor_tensor(ch, ch, over_heads(add), ALU.add))
            for h in range(2):
                ch = by_key(chunk[c[h]][:, :])
                yield step("vector", 600, ("max", u, tag, h), [("masked2", u, tag, h)],
                           lambda e, ch=ch, h=h: e.tensor_reduce(max_of(b, 0, h), ch, AX.X, ALU.max))
                yield step("vector", 600, ("shifted", u, tag, h), [("max", u, tag, h)],
                           lambda e, ch=ch, h=h: e.tensor_tensor(ch, ch, over_keys(max_of(b, 0, h)), ALU.subtract))
                yield step("scalar", 530, ("exp", u, tag, h), [("shifted", u, tag, h)],
                           lambda e, ch=ch: e.activation(ch, ch, ACT.Exp))
            slot = None
            for h in range(2):
                t = yield from turn_chunk(u, tag, v, h, b, c[h], ("exp", u, tag, h))
                if slot is None:
                    slot, free = yield Take("mixed")
                yield from mix_half(u, tag, h, b, slot, free, [(v, t)])
            yield from divided(u, tag, b, slot)

        def l1_attention(u, b, q_ready):
            at, c = {}, {}
            for h in range(2):
                at["ctx"] = yield from score(u, "ctx", h, b, q_ready)
                c[h, 0], free = yield Take("chunk")
                cc, ps = by_key(chunk[c[h, 0]][:, :]), by_key(scores[at["ctx"]][:, :])
                yield step("vector", 600, ("masked", u, "ctx", h), [("score", u, "ctx", h), ("mask_keys",), free],
                           lambda e, cc=cc, ps=ps: e.tensor_tensor(cc, ps, over_heads(mask_keys[:, u, :]), ALU.add))
                plan.free("scores", at["ctx"], ("masked", u, "ctx", h))
                yield step("vector", 600, ("max", u, "ctx", h), [("masked", u, "ctx", h)],
                           lambda e, cc=cc, h=h: e.tensor_reduce(max_of(b, 0, h), cc, AX.X, ALU.max))
                at["lat"] = yield from score(u, "lat", h, b, q_ready)
                ps = by_key(scores[at["lat"]][:, :])
                yield step("vector", 600, ("max", u, "lat", h), [("score", u, "lat", h)],
                           lambda e, ps=ps, h=h: e.tensor_reduce(max_of(b, 1, h), ps, AX.X, ALU.max))
                yield step("vector", 75, ("max", u, "both", h), [("max", u, "lat", h)],
                           lambda e, h=h: e.tensor_tensor(max_of(b, 0, h), max_of(b, 0, h), max_of(b, 1, h), ALU.max))
                yield step("gpsimd", 1250, ("shifted2", u, "ctx", h), [("max", u, "both", h)],
                           lambda e, cc=cc, h=h: e.tensor_tensor(cc, cc, over_keys(max_of(b, 0, h)), ALU.subtract))
                c[h, 1], free = yield Take("chunk")
                cl = by_key(chunk[c[h, 1]][:, :])
                yield step("vector", 600, ("shifted", u, "lat", h), [("max", u, "both", h), free],
                           lambda e, cl=cl, ps=ps, h=h: e.tensor_tensor(cl, ps, over_keys(max_of(b, 0, h)), ALU.subtract))
                plan.free("scores", at["lat"], ("shifted", u, "lat", h))
                yield step("scalar", 530, ("exp", u, "lat", h), [("shifted", u, "lat", h)],
                           lambda e, cl=cl: e.activation(cl, cl, ACT.Exp))
                yield step("scalar", 530, ("exp", u, "ctx", h), [("shifted2", u, "ctx", h)],
                           lambda e, cc=cc: e.activation(cc, cc, ACT.Exp))
            slot = None
            for h in range(2):
                tl = yield from turn_chunk(u, "lat", 1, h, b, c[h, 1], ("exp", u, "lat", h))
                tc = yield from turn_chunk(u, "lat", 0, h, b, c[h, 0], ("exp", u, "ctx", h))
                if slot is None:
                    slot, free = yield Take("mixed")
                yield from mix_half(u, "lat", h, b, slot, free, [(0, tc), (1, tl)])
            yield from divided(u, "lat", b, slot)

        def mlp(u, tag, b, w1, b1, w2, w_ready, add, out_ap):
            c = [None] * 2
            for g in range(2):
                slot, free = yield Take("work")

                def products(e, g=g, slot=slot):
                    for j in range(4):
                        for k in range(KH):
                            last = e.matmul(work[slot][:, j * P:(j + 1) * P], w1[:, k, (4 * g + j) * P:(4 * g + j + 1) * P],
                                            b.xT[:, k, :], start=(k == 0), stop=(k == KH - 1))
                    return last
                yield step("tensor", 1744, ("hid_mm", u, tag, g), [("xT", u, tag), free] + w_ready, products)
                c[g], c_free = yield Take("chunk")

                def gelu(e, g=g, slot=slot):
                    for j in range(4):
                        last = e.activation(chunk[c[g]][:, j * P:(j + 1) * P], work[slot][:, j * P:(j + 1) * P],
                                            ACT.Gelu_apprx_tanh, bias=b1[:, 4 * g + j:4 * g + j + 1])
                    return last
                yield step("scalar", 1150, ("hid", u, tag, g), [("hid_mm", u, tag, g), c_free], gelu)
                plan.free("work", slot, ("hid", u, tag, g))
            tiles = [(g, chunk[c[g]][:, j * P:(j + 1) * P], w2[:, 4 * g + j, :]) for g in range(2) for j in range(4)]
            yield from projected(u, tag, tiles, {0: [("hid", u, tag, 0)], 1: [("hid", u, tag, 1)]}, add, out_ap)
            for g in range(2):
                plan.free("chunk", c[g], ("proj_mm", u, tag, 1))

        def from_xT(b, wt):
            return [(0, b.xT[:, k, :], wt[:, k, :]) for k in range(KH)]

        def unit(u, b):
            s = u % STREAMS
            tok = slice(u * P, (u + 1) * P)
            loaded = (f"ld_unit{s}", u)
            stored = [(f"store{s}", u - STREAMS)] if u >= STREAMS else []

            yield from normed(u, "self", b, b.xin[:, :], [loaded], L0_EPS, True)
            yield from features(u, "self", [(w["qkv"], 0, 4, b.xT)], b.qk[:, :, :], folded[:, 0:4],
                                [("xT", u, "self"), ("scale_w", "sq"), ("scale_w", "skv"), ("fold_add", "sq", 1), ("fold_add", "skv")])
            yield from spread_keys(u, "self", b.qk[:, KH:, :], [("feat", u, "self")], "own_keys")
            yield from values(u, ("self", 0), b, 0, w["qkv"], 2 * H, b.xT, [])
            yield plus_bias(u, "self", b.xb[:, :], b.xin[:, :], "b_ao", [loaded, ("through_add", "ao")] + stored)
            yield from l0_attention(u, "self", 0, b, mask_self[:, :], add_self[:, :], [("add_self",)],
                                    [("feat", u, "self")])
            yield from projected(u, "self", from_xT(b, w["ao"]), {0: [("xT", u, ("self", "heads")), ("ld_w_ao",)]},
                                 b.xb[:, :], b.x[:, :])

            yield from normed(u, "cross", b, b.x[:, :], [("proj", u, "self")], L0_EPS, True)
            yield plus_bias(u, "cross", b.xb[:, :], b.x[:, :], "b_co", [("proj", u, "self"), ("through_add", "co")])
            yield from features(u, "cross", [(w["q"], 0, 2, b.xT)], b.qk[:, 0:KH, :], folded[:, 6:8],
                                [("xT", u, "cross"), ("scale_w", "cq"), ("fold_add", "cq", 1)])
            yield from l0_attention(u, "cross", 1, b, b.mask[:, :], b.add[:, :], [("add_cross", u)],
                                    [("feat", u, "cross")])
            yield from projected(u, "cross", from_xT(b, w["co"]), {0: [("xT", u, ("cross", "heads")), ("ld_w_co",)]},
                                 b.xb[:, :], b.x[:, :])

            yield from normed(u, "mlp0", b, b.x[:, :], [("proj", u, "cross")], L0_EPS, True)
            yield plus_bias(u, "mlp0", b.xb[:, :], b.x[:, :], "b2", [("proj", u, "cross")])
            yield from mlp(u, "mlp0", b, w["m1"], folded[:, 8:16], w["m2"],
                           [("scale_w", "m1"), ("fold_add", "m1"), ("ld_w_m2",)], b.xb[:, :], b.x[:, :])

            yield from turned(u, "lat", b, b.x[:, :], [("proj", u, "mlp0")])
            yield from features(u, "lat_k", [(w["lk"], 0, 2, b.xT)], b.qk[:, KH:, :], col("k_b", 0, 2),
                                [("xT", u, "lat"), ("ld_w_lk",)])
            yield from spread_keys(u, "lat", b.qk[:, KH:, :], [("feat", u, "lat_k")], "own_keys")
            yield plus_bias(u, "lat", b.xb[:, :], b.x[:, :], "out_b", [("proj", u, "mlp0"), ("through_add", "lo")])
            yield from features(u, "lat_q", [(w["lq"], 0, 2, b.xT)], b.qk[:, 0:KH, :], col("q_b", 0, 2),
                                [("scale_w", "lq"), ("scale_lqb",)])
            yield from values(u, ("lat", 1), b, 1, w["lv"], 0, b.xT, [("ld_w_lv",)])
            yield from l1_attention(u, b, [("feat", u, "lat_q")])
            yield from projected(u, "lat", from_xT(b, w["lo"]), {0: [("xT", u, ("lat", "heads")), ("ld_w_lo",)]},
                                 b.xb[:, :], b.xb[:, :])

            yield from normed(u, "mlp1", b, b.xb[:, :], [("proj", u, "lat")], L1_EPS, False)
            yield plus_bias(u, "mlp1", b.x[:, :], b.x[:, :], "mlp_b2", [("plus_bias", u, "lat"), ("turn", u, "lat")])
            yield from mlp(u, "mlp1", b, w["n1"], col("mlp_b1", 0, 8), w["n2"],
                           [("scale_w", "n1"), ("ld_w_n2",)], b.x[:, :], b.xb[:, :])
            yield dma((f"store{s}", u), [("proj", u, "mlp1")], [(out[tok, :], b.xb[:, :])])

        def context(u, b):
            s, before = u % STREAMS, u - STREAMS
            tok = slice(u * P, (u + 1) * P)
            read = [] if before < 0 else [("xn", before, "self"), ("plus_bias", before, "self"),
                                          ("masked", before, "cross", 1), ("val_mm", before, ("lat", 0))]
            yield dma((f"ld_unit{s}", u), read,
                      [(b.xin[:, :], x_in[tok, :]), (b.ctxT[:, :, :], ctxT_in[u]), (b.mask[:, :], mask_cross_in[tok, :])])
            loaded = (f"ld_unit{s}", u)
            mixed_before = [] if before < 0 else [("mix", before, "lat", 1)]
            yield step("gpsimd", 250, ("add_cross", u), [loaded],
                       lambda e: e.tensor_scalar(b.add[:, :], b.mask[:, :], -1.0, 10000.0, ALU.add, ALU.mult))
            yield from features(u, "cross_k", [(w["kv"], 0, 2, b.ctxT)], b.kc[:, :, :], col("b_kv", 0, 2),
                                [loaded, ("ld_w_kv",)] + mixed_before)
            yield from values(u, ("cross", 1), b, 1, w["kv"], H, b.ctxT, [])
            yield from spread_keys(u, "cross", b.kc[:, :, :], [("feat", u, "cross_k"), ("score", u, "self", 0)], "ctx_keys")
            yield from features(u, "ctx_k", [(w["lk"], 0, 2, b.ctxT)], b.kc[:, :, :], col("k_b", 0, 2),
                                [("ld_w_lk",), (f"place_keys_cross{s}", u), ("score", u, "cross", 1)])
            yield from values(u, ("lat", 0), b, 0, w["lv"], 0, b.ctxT, [("ld_w_lv",), ("mix", u, "self", 1)])
            yield from spread_keys(u, "ctx", b.kc[:, :, :], [("feat", u, "ctx_k"), ("xn", u, "mlp0")], "ctx_keys")

        def stream(s, part):
            for u in range(s, UNITS, STREAMS):
                yield from part(u, bufs[s])

        plan.weave([constants(), setup(), folds()] + [stream(s, part) for part in (unit, context) for s in range(STREAMS)])

        block = ctx.enter_context(nc.Block())

        @block.tensor
        def _(eng):
            for run in plan.queues["tensor"]:
                run(eng)

        @block.vector
        def _(eng):
            for run in plan.queues["vector"]:
                run(eng)

        @block.scalar
        def _(eng):
            for run in plan.queues["scalar"]:
                run(eng)

        @block.gpsimd
        def _(eng):
            for run in plan.queues["gpsimd"]:
                run(eng)

        @block.sync
        def _(eng):
            for run in plan.queues["sync"]:
                run(eng)
            for s in range(STREAMS):
                eng.wait_ge(plan.sems[f"store{s}"], plan.count[f"store{s}"])


def kernel(**inputs):
    import concourse.bacc as bacc
    from concourse.bass_utils import run_bass_kernel_spmd as launch

    a = {k: np.ascontiguousarray(v) for k, v in inputs.items()}
    l0 = lambda n: a["L0_xattn_" + n]
    l1 = lambda n: a["L1_xattn_" + n]

    def columns(v):
        return v.reshape(-1, P).T

    kv_w = l1("kv_w").reshape(H, H, 2)
    kv_b = l1("kv_b").reshape(H, 2)
    cols = {"ln1_s": l0("ln1_s"), "ln1_b": l0("ln1_b"), "b_qkv": l0("b_qkv"), "ln2_s": l0("ln2_s"),
            "ln2_b": l0("ln2_b"), "b_q": l0("b_q"), "b_kv": l0("b_kv"), "ln3_s": l0("ln3_s"),
            "ln3_b": l0("ln3_b"), "b1": l0("b1"), "q_b": l1("q_b"), "k_b": kv_b[:, 0], "v_b": kv_b[:, 1],
            "postnorm_w": l1("postnorm_w"), "mlp_b1": l1("mlp_b1")}
    rows = {"b_ao": l0("b_ao"), "b_co": l0("b_co"), "b2": l0("b2"), "out_b": l1("out_b"), "mlp_b2": l1("mlp_b2")}
    weights = {"qkv": l0("w_qkv"), "ao": l0("w_ao"), "q": l0("w_q"), "kv": l0("w_kv"), "co": l0("w_co"),
               "m1": l0("w1"), "m2": l0("w2"), "lq": l1("q_w"), "lk": kv_w[:, :, 0], "lv": kv_w[:, :, 1],
               "lo": l1("out_w"), "n1": l1("mlp_w1"), "n2": l1("mlp_w2")}
    arrays = {
        "x": a["x"].reshape(B * S, H),
        "ctxT": a["ctx_2048"].reshape(UNITS, P, KH, P).transpose(0, 3, 2, 1),
        "mask_self": a["mask_1x1xSxS2_fc1"].reshape(S, S),
        "mask_cross": a["mask_Bx1xSxS2_ff1"].reshape(B * S, S),
        "mask_keys": a["mask_BxS2_ik0"],
        "cols": np.concatenate([columns(cols[n]) for n in COLS], axis=1),
        "rows": np.stack([rows[n] for n in ROWS])[None],
    }
    arrays.update({"w_" + n: v for n, v in weights.items()})
    arrays = {k: np.ascontiguousarray(v) for k, v in arrays.items()}

    nc = bacc.Bacc("TRN2", target_bir_lowering=False, num_devices=1)
    d = {k: nc.dram_tensor("in_" + k, v.shape, mybir.dt.from_np(v.dtype), kind="ExternalInput").ap()
         for k, v in arrays.items()}
    out = nc.dram_tensor("out", (B * S, H), F32, kind="ExternalOutput").ap()
    build(nc, d["x"], d["ctxT"], d["mask_self"], d["mask_cross"], d["mask_keys"], d["cols"], d["rows"],
          {n: d["w_" + n] for n in weights}, out)
    r = launch(nc, [{"in_" + k: v for k, v in arrays.items()}], core_ids=[0])
    return r.results[0]["out"].reshape(B, S, H)
```

```python
from contextlib import ExitStack

import numpy as np

import concourse.bass as bass
from concourse import mybir

F32 = mybir.dt.float32
F16 = mybir.dt.float16
I32 = mybir.dt.int32
ALU = mybir.AluOpType
ACT = mybir.ActivationFunctionType
AX = mybir.AxisListType

P = 128
B, S, H = 64, 64, 256
NH = 16
HD = H // NH
KH = H // P
HB = P // HD
NP = NH // 2
FF = 4 * H
NF = FF // P
BU = P // S
UNITS = B // BU
STREAMS = 6
HH = NH // 2
SCORE_BANKS, MIXED_BANKS = 2, 1
OWN_KEYS, CTX_KEYS = 2, 2
CHUNKS, TURNED_CHUNKS = 8, 4
STAGED = KH * FF // 512
VW = 2 * (HD + 1)
L0_EPS, L1_EPS = 1e-5, 1e-6
L0_SCALE = float(HD) ** -0.5
L1_SCALE = 1.0 / HD

SEEN = {"tensor": 320, "vector": 250, "scalar": 230, "gpsimd": 150, "sync": 100}
SEEN_OWN = {"tensor": 60, "vector": 200, "scalar": 200, "gpsimd": 100, "sync": 100}
DMA_HOLD, DMA_DONE = 656, 1700
TABLES = ("exp", "hid")
TABLE_NS = 1000
AGE = 30
AGE_LAST = 24
TIE = 10

XHAT_UP, W_TOP = 11, 13
HALVED = {"qkv": 0, "q": 1, "m1": 2, "n1": 3, "m2": 4, "n2": 5}
HIDDEN_OF = {"m2": "m1", "n2": "n1"}
HIDDEN_TOP = 14
F32_BIAS, F32_MANTISSA = 127, 23
MASKED = -1e30

COLS = {}
for _name, _n in (("ln1_s", 2), ("ln1_b", 2), ("b_qkv", 6), ("ln2_s", 2), ("ln2_b", 2), ("b_q", 2),
                  ("b_kv", 4), ("ln3_s", 2), ("ln3_b", 2), ("b1", 8), ("q_b", 2), ("k_b", 2),
                  ("v_b", 2), ("postnorm_w", 2), ("mlp_b1", 8)):
    COLS[_name] = (sum(n for _, n in COLS.values()), _n)
NCOLS = sum(n for _, n in COLS.values())
ROWS = {n: i for i, n in enumerate(("b_ao", "b_co", "b2", "out_b", "mlp_b2"))}


class Step:

    def __init__(self, engine, ns, name, after, emit, dmas=0):
        self.engine, self.ns, self.name, self.emit, self.dmas = engine, ns, name, emit, dmas
        self.table = name[0] if name[0] in TABLES else None
        self.unit = name[1] if len(name) > 1 and isinstance(name[1], int) else 0
        self.after = [k for k in after if k is not None]


class Take:

    def __init__(self, pool, engine, after):
        self.pool, self.engine, self.ns, self.table = pool, engine, 0, None
        self.unit = max([k[1] for k in after if k and len(k) > 1 and isinstance(k[1], int)], default=0)
        self.after = [k for k in after if k is not None]


class Behind:

    def __init__(self, key):
        self.key = key


class Plan:

    def __init__(self, nc, ctx):
        self.nc, self.ctx = nc, ctx
        self.queues = {e: [] for e in ("sync", "gpsimd", "scalar", "vector", "tensor")}
        self.sems, self.count, self.value, self.owner = {}, {}, {}, {}
        self.waited = {e: {} for e in self.queues}
        self.engine_free = {e: 0.0 for e in self.queues}
        self.at = {}
        self.table = None
        self.pools = {}

    def add(self, step):
        kind = step.name[0]
        assert self.owner.setdefault(kind, step.engine) == step.engine, kind
        if kind not in self.sems:
            self.sems[kind] = self.ctx.enter_context(self.nc.semaphore("s_" + kind))
            self.count[kind] = 0
        waits = []
        for key in step.after:
            v = self.value[key]
            if self.waited[step.engine].get(key[0], 0) < v:
                self.waited[step.engine][key[0]] = v
                waits.append((self.sems[key[0]], v))
        dmas = step.dmas
        self.count[kind] += 16 * dmas if dmas else 1
        self.value[step.name] = self.count[kind]
        sem = self.sems[kind]

        def run(eng):
            for s, v in waits:
                eng.wait_ge(s, v)
            last = step.emit(eng)
            if dmas:
                assert len(last) == dmas
                for i in last:
                    i.then_inc(sem, 16)
            else:
                last.then_inc(sem, 1)
        self.queues[step.engine].append(run)
        start = self.start(step)
        if step.table:
            self.table = step.table
        self.engine_free[step.engine] = start + (DMA_HOLD * dmas or step.ns + (30 if step.engine == "tensor" else 0))
        self.at[step.name] = start + (DMA_DONE + DMA_HOLD * dmas if dmas else step.ns), step.engine

    def start(self, step):
        ready = self.engine_free[step.engine]
        for k in step.after:
            at, engine = self.at[k]
            ready = max(ready, at + (SEEN_OWN if engine == step.engine else SEEN)[step.engine])
        return ready + (TABLE_NS if step.table and step.table != self.table else 0)

    def known(self, step):
        return all(k in self.value for k in step.after)

    def slot_free(self, slot):
        return self.at[slot[1]][0] if slot[1] else 0

    def pool(self, name, slots):
        self.pools[name] = [(i, None) for i in range(slots)]

    def free(self, name, slot, key):
        self.pools[name].append((slot, key))

    def weave(self, streams):
        heads = [(next(s), s) for s in streams]

        def go_on(n, value=None):
            s = heads[n][1]
            try:
                heads[n] = (s.send(value), s)
            except StopIteration:
                heads[n] = (None, s)

        while any(head is not None for head, _ in heads):
            best = None
            for n in range(len(heads)):
                while isinstance(heads[n][0], Behind) and heads[n][0].key in self.value:
                    go_on(n)
                head = heads[n][0]
                if not isinstance(head, (Step, Take)) or not self.known(head):
                    continue
                t = self.start(head) + AGE * min(head.unit, AGE_LAST)
                if isinstance(head, Take):
                    if not self.pools[head.pool]:
                        continue
                    t = max(t, min(map(self.slot_free, self.pools[head.pool])) + SEEN[head.engine] + AGE * min(head.unit, AGE_LAST))
                if best is None or t < best[0] - TIE:
                    best = (t, n)
            assert best is not None, [h.pool if isinstance(h, Take) else h.key if isinstance(h, Behind) else (h and h.name, h and h.after) for h, _ in heads]
            n = best[1]
            if isinstance(heads[n][0], Take):
                pool = self.pools[heads[n][0].pool]
                slot = min(pool, key=self.slot_free)
                pool.remove(slot)
                go_on(n, slot)
            if isinstance(heads[n][0], Step) and self.known(heads[n][0]):
                self.add(heads[n][0])
                go_on(n)


def build(nc, x_in, ctxT_in, mask_self_in, mask_cross_in, mask_keys_in, cols_in, rows_in, weights_in,
          out):
    with ExitStack() as ctx:
        def sb(name, shape, dt=F32):
            return ctx.enter_context(nc.sbuf_tensor(name, shape, dt))

        plan = Plan(nc, ctx)

        def banks(name, n):
            plan.pool(name, n)
            return [ctx.enter_context(nc.psum_tensor(f"{name}{i}", [P, 512], F32)) for i in range(n)]

        scores = banks("scores", SCORE_BANKS)
        mixed = banks("mixed", MIXED_BANKS)
        work = banks("work", 8 - SCORE_BANKS - MIXED_BANKS)

        chunks = sb("chunks", [P, CHUNKS, 512])
        turned_chunks = sb("turned_chunks", [P, TURNED_CHUNKS, 4, P])
        stage = chunks[:, 0:STAGED, :].rearrange("p c n -> p (c n)").rearrange("p (k n) -> p k n", k=KH)
        stage_deep = chunks[:, 0:STAGED, :].rearrange("p c n -> p (c n)").rearrange("p (k n) -> p k n", k=NF)
        stage_q = turned_chunks[:, 0, :, :].rearrange("p c n -> p (c n)").rearrange("p (k n) -> p k n", k=KH)
        w, w_hi, w_lo = {}, {}, {}
        for name, ap in weights_in.items():
            shape = [P, ap.shape[0] // P, ap.shape[1]]
            if name in HALVED:
                w[name] = stage_q if name == "q" else stage_deep if name in HIDDEN_OF else stage[:, :, 0:ap.shape[1]]
                w_hi[name], w_lo[name] = sb("hi_" + name, shape, F16), sb("lo_" + name, shape, F16)
            else:
                w[name] = sb("w_" + name, shape)
        largest = sb("largest", [P, len(HALVED)])
        exponent = sb("exponent", [P, 3], I32)
        hidden_up = sb("hidden_up", [P, len(HALVED)])
        most = sb("most", [P, 1])
        up, down = sb("up", [P, len(HALVED)]), sb("down", [P, len(HALVED)])
        ones_row = sb("ones_row", [1, P])
        cols = sb("cols", [P, NCOLS])
        rows = sb("rows", [P, len(ROWS), H])
        folded = sb("folded", [P, 16])
        spread_bias = sb("spread_bias", [P, KH, P])
        ident = sb("ident", [P, P])
        minus_half = sb("minus_half", [P, 1])
        mask_self = sb("mask_self", [P, S])
        add_self = sb("add_self", [P, S])

        spread = [sb(f"spread{i}", [P, KH, HB, P]) for i in range(OWN_KEYS + CTX_KEYS)]
        plan.pools["own_keys"] = [(i, None) for i in range(OWN_KEYS)]
        plan.pools["ctx_keys"] = [(OWN_KEYS + i, None) for i in range(CTX_KEYS)]

        chunk = [chunks[:, i, :] for i in range(CHUNKS)]
        plan.pools["chunk"] = [(i, None) for i in range(STAGED, CHUNKS)]
        turned_chunk = [turned_chunks[:, i, :, :] for i in range(TURNED_CHUNKS)]
        plan.pools["turned_chunk"] = [(i, None) for i in range(1, TURNED_CHUNKS)]

        spread_at = {}

        class Buffers:
            pass

        bufs = []
        for s in range(STREAMS):
            b = Buffers()
            b.xin = sb(f"xin{s}", [P, H])
            b.x = sb(f"x{s}", [P, H])
            b.xb = sb(f"xb{s}", [P, H])
            b.xn = sb(f"xn{s}", [P, H])
            b.xT = sb(f"xT{s}", [P, KH, P])
            halves_of_x = b.xT[:, :, :].bitcast(F16).rearrange("p k t -> p (k t)").rearrange("p (i k t) -> p i k t", i=2, k=KH)
            b.x_hi, b.x_lo = halves_of_x[:, 0, :, :], halves_of_x[:, 1, :, :]
            b.ctxT = sb(f"ctxT{s}", [P, KH, P])
            b.qk = sb(f"qk{s}", [P, 2 * KH, P])
            b.kc = sb(f"kc{s}", [P, KH, P])
            b.val = [sb(f"val{s}_{i}", [P, BU, NP, VW]) for i in range(2)]
            b.mask = sb(f"mask{s}", [P, S])
            b.add = sb(f"add{s}", [P, S])
            b.keys_i = sb(f"keys_i{s}", [P, S], I32)
            b.keys = sb(f"keys{s}", [P, S])
            b.bn = sb(f"bn{s}", [P, 6])
            b.mv = sb(f"mv{s}", [P, 2])
            b.var = sb(f"var{s}", [P, 1])
            b.rstd = sb(f"rstd{s}", [P, 1])
            b.mx = [sb(f"mx{s}_{i}", [P, NH]) for i in range(2)]
            b.rs = sb(f"rs{s}", [P, NH])
            bufs.append(b)

        def col(name, i=0, n=1):
            c = COLS[name][0] + i
            return cols[:, c:c + n]

        def step(engine, ns, name, after, emit):
            return Step(engine, ns, name, after, emit)

        def dma(name, after, pairs):
            return Step("sync", 0, name, after, lambda eng: [eng.dma_start(o, i) for o, i in pairs],
                        dmas=len(pairs))

        def setup():
            yield dma(("ld_cols",), [], [(cols[:, :], cols_in)])
            staged_before = {"m1": [("lo", "qkv")], "m2": [("lo", "m1")], "n1": [("lo", "m2")], "n2": [("lo", "n1")]}

            def load(name):
                return dma((f"ld_w_{name}",), staged_before.get(name, []),
                           [(w[name][:, :, :], weights_in[name].rearrange("(k p) n -> p k n", p=P))])
            yield load("qkv")
            yield load("kv")
            yield Behind((f"ld_unit{STREAMS - 1}", STREAMS - 1))
            yield dma(("ld_rows",), [], [(rows[:, :, :], rows_in.broadcast_to([P, len(ROWS), H]))])
            yield dma(("ld_mask_self",), [], [(mask_self[S * b:S * b + S, :], mask_self_in) for b in range(BU)])
            for name in ("ao", "q", "co", "lk", "lv", "lq", "lo", "m1", "m2", "n1", "n2"):
                yield load(name)

        def constants():
            yield step("gpsimd", 200, ("ident0",), [], lambda e: e.memset(ident[:, :], 0.0))
            yield step("gpsimd", 200, ("ident",), [("ident0",)],
                       lambda e: e.affine_select(out=ident[:, :], in_=ident[:, :], compare_op=ALU.not_equal,
                                                 fill=1.0, base=0, pattern=[[-1, P]], channel_multiplier=1))
            yield step("gpsimd", 100, ("minus_half",), [], lambda e: e.memset(minus_half[:, :], -0.5))
            yield step("gpsimd", 100, ("ones_row",), [], lambda e: e.memset(ones_row[:, :], 1.0))
            for s in range(STREAMS):
                for i in range(2):
                    v = bufs[s].val[i]
                    yield step("vector", 600, ("val0", s, i), [], lambda e, v=v: e.memset(v[:, :, :, :], 0.0))

                    def ones(e, v=v):
                        for half in range(2):
                            last = e.memset(v[S * half:S * half + S, :, :, half * (HD + 1) + HD:half * (HD + 1) + HD + 1], 1.0)
                        return last
                    yield step("vector", 200, ("val1", s, i), [("val0", s, i)], ones)
            for i in range(OWN_KEYS + CTX_KEYS):
                yield step("gpsimd", 2200, ("spread0", i), [], lambda e, i=i: e.memset(spread[i][:, :, :, :], 0.0))

        def fold(name, wname, first, tiles, beta, at, bias, scale):
            slot, free = yield Take("work", "tensor", [("ld_w_" + wname,), ("ld_cols",)])

            def products(e):
                for f in range(tiles):
                    for k in range(KH):
                        last = e.matmul(work[slot][:, f:f + 1], w[wname][:, k, (first + f) * P:(first + f + 1) * P],
                                        col(beta, k), start=(k == 0), stop=(k == KH - 1))
                return last
            yield step("tensor", 900 * tiles, ("fold_mm", name), [("ld_w_" + wname,), ("ld_cols",), free], products)
            yield step("vector", 100, ("fold_add", name), [("fold_mm", name)],
                       lambda e: e.tensor_tensor(folded[:, at:at + tiles], work[slot][:, 0:tiles],
                                                 col(bias[0], bias[1], tiles), ALU.add))
            plan.free("work", slot, ("fold_add", name))
            if scale != 1.0:
                yield step("vector", 100, ("fold_add", name, 1), [("fold_add", name)],
                           lambda e: e.tensor_scalar(folded[:, at:at + tiles], folded[:, at:at + tiles],
                                                     scale, None, ALU.mult))

        def scale_rows(key, wname, lo, hi, s_col, scale, after):
            def emit(e):
                for k in range(KH):
                    a = w[wname][:, k, lo:hi]
                    if s_col is None:
                        last = e.tensor_scalar(a, a, scale, None, ALU.mult)
                    else:
                        last = e.tensor_scalar(a, a, col(s_col, k), scale, ALU.mult, ALU.mult)
                return last
            return step("vector", 300 * KH, ("scale_w", key), after + [("ld_w_" + wname,), ("ld_cols",)], emit)

        def through(name, wname, src, row, after):
            yield step("vector", 400, ("spread_bias", name), after,
                       lambda e: e.tensor_copy(spread_bias[:, :, :], src.unsqueeze(2).broadcast_to([P, KH, P])))
            slot, free = yield Take("work", "tensor", [("spread_bias", name), ("ld_w_" + wname,)])

            def products(e):
                for k in range(KH):
                    last = e.matmul(work[slot][:, 0:H], spread_bias[:, k, :], w[wname][:, k, :],
                                    start=(k == 0), stop=(k == KH - 1))
                return last
            yield step("tensor", 900, ("through_mm", name), [("spread_bias", name), ("ld_w_" + wname,), free], products)
            r = rows[:, ROWS[row], :]
            yield step("vector", 350, ("through_add", name), [("through_mm", name), ("ld_rows",)],
                       lambda e: e.tensor_tensor(r, r, work[slot][:, 0:H], ALU.add))
            plan.free("work", slot, ("through_add", name))

        def everywhere(name, at, after):
            slot, free = yield Take("work", "tensor", after + [("ident",)])
            row = work[slot][0:1, 0:P]
            yield step("tensor", 110, ("largest_row", name), after + [("ident",), free],
                       lambda e: e.transpose(row, at, ident[:, :]))
            yield step("vector", 200, ("largest_all", name), [("largest_row", name)],
                       lambda e: e.tensor_reduce(at[0:1, :], row, AX.X, ALU.max))
            yield step("tensor", 110, ("largest_everywhere", name), [("largest_all", name), ("ones_row",)],
                       lambda e: e.matmul(work[slot][:, P:P + 1], ones_row[:, :], at[0:1, :], start=True, stop=True))
            yield step("vector", 75, ("largest_here", name), [("largest_everywhere", name)],
                       lambda e: e.tensor_copy(at, work[slot][:, P:P + 1]))
            plan.free("work", slot, ("largest_here", name))

        def on_exponents(name, after, ops):
            for i, (o, a, s1, s2, op0, op1) in enumerate(ops):
                more = {} if op1 is None else {"op1": op1}
                yield step("vector", 75, ("top", name, i + 1), [("top", name, i)] if i else after,
                           lambda e, o=o, a=a, s1=s1, s2=s2, op0=op0, more=more: e.tensor_scalar(o, a, s1, s2, op0, **more))

        def power(to, bound, ex, top, reach):
            return [(ex, bound.bitcast(I32), F32_MANTISSA, None, ALU.logical_shift_right, None),
                    (ex, ex, -1, 2 * F32_BIAS + top, ALU.mult, ALU.add),
                    (ex, ex, F32_BIAS + reach, F32_BIAS - reach, ALU.min, ALU.max),
                    (to.bitcast(I32), ex, F32_MANTISSA, None, ALU.logical_shift_left, None)]

        def halves(name, after):
            c = HALVED[name]
            most_at = largest[:, c:c + 1]
            yield step("vector", 1100 * KH, ("largest", name), after,
                       lambda e: e.tensor_reduce(most_at, w[name][:, :, :], AX.XY, ALU.max, apply_absolute_value=True))
            yield from everywhere(name, most_at, [("largest", name)])
            ex_up, ex_down, ex_hidden = (exponent[:, i:i + 1] for i in range(3))
            ops = power(up[:, c:c + 1], most_at, ex_up, W_TOP, 60)
            if name in HIDDEN_OF:
                ops += [(ex_down, ex_hidden, -1, 3 * F32_BIAS, ALU.mult, ALU.add)]
            else:
                ops += [(ex_down, ex_up, -1, 2 * F32_BIAS - XHAT_UP, ALU.mult, ALU.add)]
            yield from on_exponents(name, [("largest_here", name)], ops)
            last = ("top", name, len(ops))
            if name in HIDDEN_OF:
                yield step("vector", 75, ("ex_down", name), [last],
                           lambda e: e.tensor_tensor(ex_down, ex_down, ex_up, ALU.subtract))
                last = ("ex_down", name)
            yield step("vector", 75, ("down", name), [last],
                       lambda e: e.tensor_scalar(down[:, c:c + 1].bitcast(I32), ex_down, F32_MANTISSA, None, ALU.logical_shift_left))
            yield step("scalar", 900 * KH, ("hi", name), [("down", name)],
                       lambda e: e.activation(w_hi[name][:, :, :], w[name][:, :, :], ACT.Copy, scale=up[:, c:c + 1]))
            yield step("vector", 1100 * KH, ("lo", name), [("hi", name)],
                       lambda e: e.scalar_tensor_tensor(w_lo[name][:, :, :], w[name][:, :, :], up[:, c:c + 1],
                                                        w_hi[name][:, :, :], ALU.mult, ALU.subtract))

        def hidden_scale(name, bias, after):
            c, at, tag = HALVED[name], most[:, 0:1], "hidden_" + name
            yield step("vector", 75, ("bias_most", name), after,
                       lambda e: e.tensor_reduce(at, bias, AX.X, ALU.max, apply_absolute_value=True))
            yield step("vector", 75, ("bound", name), [("bias_most", name), ("largest_here", name)],
                       lambda e: e.scalar_tensor_tensor(at, largest[:, c:c + 1], float(H), at, ALU.mult, ALU.add))
            yield from everywhere(tag, at, [("bound", name)])
            yield from on_exponents(tag, [("largest_here", tag)],
                                    power(hidden_up[:, c:c + 1], at, exponent[:, 2:3], HIDDEN_TOP, 60))

        def folds():
            yield from fold("sq", "qkv", 0, 2, "ln1_b", 0, ("b_qkv", 0), L0_SCALE)
            yield from fold("skv", "qkv", 2, 4, "ln1_b", 2, ("b_qkv", 2), 1.0)
            yield scale_rows("sq", "qkv", 0, H, "ln1_s", L0_SCALE, [("fold_mm", "skv")])
            yield scale_rows("skv", "qkv", H, 3 * H, "ln1_s", 1.0, [("fold_mm", "skv")])
            yield from halves("qkv", [("scale_w", "sq"), ("scale_w", "skv")])
            yield step("vector", 150, ("add_self",), [("ld_mask_self",)],
                       lambda e: e.tensor_scalar(add_self[:, :], mask_self[:, :], 1.0, 10000.0, ALU.subtract, ALU.mult))
            yield from through("ao", "ao", folded[:, 4:6], "b_ao", [("fold_add", "skv")])
            yield from fold("cq", "q", 0, 2, "ln2_b", 6, ("b_q", 0), L0_SCALE)
            yield scale_rows("cq", "q", 0, H, "ln2_s", L0_SCALE, [("fold_mm", "cq")])
            yield from halves("q", [("scale_w", "cq")])
            plan.free("turned_chunk", 0, ("lo", "q"))
            yield from through("co", "co", col("b_kv", 2, 2), "b_co", [("through_mm", "ao")])
            yield scale_rows("lq", "lq", 0, H, None, L1_SCALE, [])
            yield step("vector", 100, ("scale_lqb",), [("ld_cols",)],
                       lambda e: e.tensor_scalar(col("q_b", 0, 2), col("q_b", 0, 2), L1_SCALE, None, ALU.mult))
            yield from through("lo", "lo", col("v_b", 0, 2), "out_b", [("through_mm", "co")])
            yield from fold("m1", "m1", 0, 8, "ln3_b", 8, ("b1", 0), 1.0)
            yield scale_rows("m1", "m1", 0, FF, "ln3_s", 1.0, [("fold_mm", "m1")])
            yield from halves("m1", [("scale_w", "m1")])
            yield from hidden_scale("m1", folded[:, 8:16], [("fold_add", "m1")])
            yield from halves("m2", [("ld_w_m2",)])
            yield scale_rows("n1", "n1", 0, FF, "postnorm_w", 1.0, [])
            yield from halves("n1", [("scale_w", "n1")])
            yield from hidden_scale("n1", col("mlp_b1", 0, 8), [("ld_cols",)])
            yield from halves("n2", [("ld_w_n2",)])
            for i in range(STAGED):
                plan.free("chunk", i, ("lo", "n2"))

        def normed(u, tag, b, src, src_ready, eps, centred):
            shrink = 2.0 ** (-2 * XHAT_UP)
            k = lambda n: (n, u, tag)
            yield step("vector", 340, k("bn_stats"), src_ready, lambda e: e.bn_stats(b.bn[:, :], src))
            yield step("vector", 75, k("bn_aggr"), [k("bn_stats")], lambda e: e.bn_aggr(b.mv[:, :], b.bn[:, :]))
            if centred:
                yield step("vector", 70, k("var_eps"), [k("bn_aggr")],
                           lambda e: e.tensor_scalar(b.var[:, :], b.mv[:, 1:2], eps, shrink, ALU.add, ALU.mult))
            else:
                yield step("vector", 130, k("mean_square"), [k("bn_aggr")],
                           lambda e: e.scalar_tensor_tensor(b.rs[:, 0:1], b.mv[:, 0:1], b.mv[:, 0:1], b.mv[:, 1:2],
                                                            ALU.mult, ALU.add))
                yield step("vector", 70, k("var_eps"), [k("mean_square")],
                           lambda e: e.tensor_scalar(b.var[:, :], b.rs[:, 0:1], eps, shrink, ALU.add, ALU.mult))
            yield step("gpsimd", 450, k("rstd"), [k("var_eps"), ("minus_half",)],
                       lambda e: e.tensor_tensor(b.rstd[:, :], b.var[:, :], minus_half[:, :], ALU.pow))
            if centred:
                yield step("vector", 323, k("xn"), [k("rstd")],
                           lambda e: e.tensor_scalar(b.xn[:, :], src, b.mv[:, 0:1], b.rstd[:, 0:1],
                                                     ALU.subtract, ALU.mult))
            else:
                yield step("vector", 323, k("xn"), [k("rstd")],
                           lambda e: e.tensor_scalar(b.xn[:, :], src, b.rstd[:, 0:1], None, ALU.mult))
            slot = yield from turn_tokens(u, tag, b.xn[:, :], [k("xn")])
            ps = work[slot][:, 0:KH * P].rearrange("p (k t) -> p k t", k=KH)
            yield step("scalar", 264, k("x_hi"), [("turn", u, tag)], lambda e: e.copy(b.x_hi, ps))
            yield step("vector", 340, k("x_lo"), [k("x_hi")],
                       lambda e: e.tensor_tensor(b.x_lo, ps, b.x_hi, ALU.subtract))
            plan.free("work", slot, k("x_lo"))

        def turn_tokens(u, tag, src, src_ready):
            slot, free = yield Take("work", "tensor", src_ready + [("ident",)])

            def turn(e):
                for h in range(KH):
                    last = e.transpose(work[slot][:, h * P:(h + 1) * P], src[:, h * P:(h + 1) * P], ident[:, :])
                return last
            yield step("tensor", 220, ("turn", u, tag), src_ready + [free, ("ident",)], turn)
            return slot

        def turned(u, tag, b, src, src_ready):
            slot = yield from turn_tokens(u, tag, src, src_ready)
            yield step("scalar", 264, ("xT", u, tag), [("turn", u, tag)],
                       lambda e: e.copy(b.xT[:, :, :], work[slot][:, 0:KH * P].rearrange("p (k t) -> p k t", k=KH)))
            plan.free("work", slot, ("xT", u, tag))

        def halved_tile(e, out_ap, name, c, b):
            last, n = None, 0
            for k in range(KH):
                for wt, x in ((w_hi, b.x_hi), (w_hi, b.x_lo), (w_lo, b.x_hi)):
                    last = e.matmul(out_ap, wt[name][:, k, c:c + P], x[:, k, :], start=(n == 0), stop=(n == 3 * KH - 1))
                    n += 1
            return last

        def halved_features(u, tag, name, tiles, b, out_ap, bias, ready):
            slot, free = yield Take("work", "tensor", [("x_lo", u, tag), ("lo", name)])

            def products(e):
                for f in range(tiles):
                    last = halved_tile(e, work[slot][:, f * P:(f + 1) * P], name, f * P, b)
                return last
            yield step("tensor", 3 * 56 * KH * tiles, ("feat_mm", u, tag), [("x_lo", u, tag), ("lo", name), free], products)
            c = HALVED[name]
            yield step("vector", 130 + 134 * tiles, ("feat", u, tag), [("feat_mm", u, tag)] + ready,
                       lambda e: e.scalar_tensor_tensor(
                           out_ap, work[slot][:, 0:tiles * P].rearrange("p (f t) -> p f t", f=tiles), down[:, c:c + 1],
                           bias.unsqueeze(2).broadcast_to([P, tiles, P]), ALU.mult, ALU.add))
            plan.free("work", slot, ("feat", u, tag))

        def features(u, tag, parts, out_ap, bias, ready):
            slot, free = yield Take("work", "tensor", ready)
            n = sum(p[2] for p in parts)

            def products(e):
                f = 0
                for wt, c, tiles, xT in parts:
                    for i in range(tiles):
                        for k in range(KH):
                            last = e.matmul(work[slot][:, f * P:(f + 1) * P], wt[:, k, c + i * P:c + (i + 1) * P],
                                            xT[:, k, :], start=(k == 0), stop=(k == KH - 1))
                        f += 1
                return last
            yield step("tensor", 436 * n, ("feat_mm", u, tag), ready + [free], products)
            yield step("vector", 70 + 134 * n, ("feat", u, tag), [("feat_mm", u, tag)],
                       lambda e: e.tensor_tensor(out_ap, work[slot][:, 0:n * P].rearrange("p (f t) -> p f t", f=n),
                                                 bias.unsqueeze(2).broadcast_to([P, n, P]), ALU.add))
            plan.free("work", slot, ("feat", u, tag))

        def spread_keys(u, tag, kT, ready, pool):
            slot, free = yield Take(pool, "sync", ready + [("spread0", 0)])
            spread_at[u, tag] = pool, slot
            first = [("spread0", slot)]
            yield dma((f"place_keys_{tag}{u % STREAMS}", u), ready + first + [free],
                      [(spread[slot][HD * h:HD * h + HD, :, h, :], kT[HD * h:HD * h + HD, :, :]) for h in range(HB)])

        def values(u, tag, b, i, parts, ready, scale=None):
            slot, free = yield Take("work", "tensor", ready)

            def products(e):
                for n, (lhs, rhs) in enumerate(parts):
                    last = e.matmul(work[slot][:, 0:H], lhs, rhs, start=(n == 0), stop=(n == len(parts) - 1))
                return last
            yield step("tensor", 864 if scale is None else 6 * 109, ("val_mm", u, tag), ready + [free], products)
            v = work[slot][:, 0:H].rearrange("p (n e d) -> p n e d", n=NP, e=2)

            def place(e):
                for q in range(BU):
                    for odd in range(2):
                        c0 = odd * (HD + 1)
                        o, a = b.val[i][S * odd:S * odd + S, q, :, c0:c0 + HD], v[S * q:S * q + S, :, odd, :]
                        last = e.copy(o, a) if scale is None else \
                            e.activation(o, a, ACT.Copy, scale=scale[S * q:S * q + S, :])
                return last
            yield step("scalar", 640 if scale is None else 1000, ("val", u, tag),
                       [("val_mm", u, tag), ("val1", u % STREAMS, i)], place)
            plan.free("work", slot, ("val", u, tag))

        def plain(xT, wt, c=0):
            return [(xT[:, k, :], wt[:, k, c:c + H]) for k in range(KH)]

        def score(u, tag, h, b, q_ready):
            yield Behind((f"place_keys_{tag}{u % STREAMS}", u))
            pool, sp = spread_at[u, tag]
            slot, free = yield Take("scores", "tensor", q_ready + [(f"place_keys_{tag}{u % STREAMS}", u)])

            def products(e):
                for q in range(BU):
                    last = e.matmul(scores[slot][S * q:S * q + S, :], b.qk[:, h, S * q:S * q + S],
                                    spread[sp][:, h, :, S * q:S * q + S], start=True, stop=True)
                return last
            yield step("tensor", 879, ("score", u, tag, h),
                       q_ready + [(f"place_keys_{tag}{u % STREAMS}", u), free], products)
            if h == KH - 1:
                plan.free(pool, sp, ("score", u, tag, h))
            return slot

        def by_key(ap):
            return ap.rearrange("p (h k) -> p h k", h=HH)

        def over_heads(ap):
            return ap.unsqueeze(1).broadcast_to([P, HH, S])

        def over_keys(ap):
            return ap.unsqueeze(2).broadcast_to([P, HH, S])

        def max_of(b, i, h):
            return b.mx[i][:, HH * h:HH * h + HH]

        def turn_chunk(u, tag, i, h, b, c, ready):
            slot, free = yield Take("work", "tensor", [ready])

            def turn(e):
                for j in range(4):
                    last = e.transpose(work[slot][:, j * P:(j + 1) * P], chunk[c][:, j * P:(j + 1) * P], ident[:, :])
                return last
            yield step("tensor", 440, ("prob_turn", u, tag, i, h), [ready, free], turn)
            plan.free("chunk", c, ("prob_turn", u, tag, i, h))
            t, t_free = yield Take("turned_chunk", "scalar", [("prob_turn", u, tag, i, h)])
            src = work[slot][:, :].rearrange("p (n t) -> p n t", n=4)
            key = ("probT", u, tag, i, h)
            yield step("scalar", 480, key, [("prob_turn", u, tag, i, h), t_free],
                       lambda e: e.copy(turned_chunk[t], src))
            plan.free("work", slot, key)
            return t

        def mix_half(u, tag, h, b, slot, free, turned_at):
            def products(e):
                for q in range(BU):
                    for j in range(NP // 2):
                        p = h * (NP // 2) + j
                        for n, (i, t) in enumerate(turned_at):
                            last = e.matmul(mixed[slot][S * q:S * q + S, p * VW:(p + 1) * VW],
                                            turned_chunk[t][:, j, S * q:S * q + S], b.val[i][:, q, p, :],
                                            start=(n == 0), stop=(n == len(turned_at) - 1))
                return last
            yield step("tensor", (606, 1242)[len(turned_at) - 1], ("mix", u, tag, h),
                       [("probT", u, tag, i, h) for i, _ in turned_at]
                       + [("val", u, (tag, i)) for i, _ in turned_at] + [free], products)
            for _, t in turned_at:
                plan.free("turned_chunk", t, ("mix", u, tag, h))

        def divided(u, tag, b, slot):
            m = mixed[slot][:, 0:NP * VW].rearrange("p (h d) -> p h d", d=HD + 1)
            yield step("vector", 165, ("denominator", u, tag), [("mix", u, tag, 1)],
                       lambda e: e.reciprocal(b.rs[:, :].unsqueeze(2), m[:, :, HD:HD + 1]))
            yield step("vector", 340, ("heads", u, tag), [("denominator", u, tag)],
                       lambda e: e.tensor_tensor(b.xn[:, :].rearrange("p (h d) -> p h d", h=NH), m[:, :, 0:HD],
                                                 b.rs[:, :].unsqueeze(2).broadcast_to([P, NH, HD]), ALU.mult))
            plan.free("mixed", slot, ("heads", u, tag))
            yield from turned(u, (tag, "heads"), b, b.xn[:, :], [("heads", u, tag)])

        def projected(u, tag, tiles, ready, add, out_ap, scale=None):
            slot, free = yield Take("work", "tensor", ready[min(ready)])
            for part in sorted(ready):
                mine = [n for n, t in enumerate(tiles) if t[0] == part]

                def products(e, mine=mine):
                    for n in mine:
                        last = e.matmul(work[slot][:, 0:H], tiles[n][1], tiles[n][2], start=(n == 0), stop=(n == len(tiles) - 1))
                    return last
                yield step("tensor", (432 if scale is None else 109) * len(mine), ("proj_mm", u, tag, part), ready[part] + [free], products)
            yield step("vector", 340, ("proj", u, tag), [("proj_mm", u, tag, max(ready)), ("plus_bias", u, tag)],
                       lambda e: e.tensor_tensor(out_ap, work[slot][:, 0:H], add, ALU.add) if scale is None else
                       e.scalar_tensor_tensor(out_ap, work[slot][:, 0:H], scale, add, ALU.mult, ALU.add))
            plan.free("work", slot, ("proj", u, tag))

        def plus_bias(u, tag, out_ap, in_ap, row, ready):
            return step("gpsimd", 687, ("plus_bias", u, tag), ready,
                        lambda e: e.tensor_tensor(out_ap, in_ap, rows[:, ROWS[row], :], ALU.add))

        def l0_attention(u, tag, v, b, mask, add, mask_ready, q_ready):
            at, c = [None] * 2, [None] * 2
            for h in range(2):
                at[h] = yield from score(u, tag, h, b, q_ready)
                c[h], free = yield Take("chunk", "vector", [("score", u, tag, h)] + mask_ready)
                ch, ps = by_key(chunk[c[h]]), by_key(scores[at[h]][:, :])
                yield step("vector", 600, ("masked", u, tag, h), [("score", u, tag, h), free] + mask_ready,
                           lambda e, ch=ch, ps=ps: e.tensor_tensor(ch, ps, over_heads(mask), ALU.mult))
                plan.free("scores", at[h], ("masked", u, tag, h))
                yield step("gpsimd", 1225, ("masked2", u, tag, h), [("masked", u, tag, h)],
                           lambda e, ch=ch: e.tensor_tensor(ch, ch, over_heads(add), ALU.add))
            for h in range(2):
                ch = by_key(chunk[c[h]])
                yield step("vector", 600, ("max", u, tag, h), [("masked2", u, tag, h)],
                           lambda e, ch=ch, h=h: e.tensor_reduce(max_of(b, 0, h), ch, AX.X, ALU.max))
                yield step("vector", 600, ("shifted", u, tag, h), [("max", u, tag, h)],
                           lambda e, ch=ch, h=h: e.tensor_tensor(ch, ch, over_keys(max_of(b, 0, h)), ALU.subtract))
                yield step("scalar", 530, ("exp", u, tag, h), [("shifted", u, tag, h)],
                           lambda e, ch=ch: e.activation(ch, ch, ACT.Exp))
            slot = None
            for h in range(2):
                t = yield from turn_chunk(u, tag, v, h, b, c[h], ("exp", u, tag, h))
                if slot is None:
                    slot, free = yield Take("mixed", "tensor", [("probT", u, tag, v, h), ("val", u, (tag, v))])
                yield from mix_half(u, tag, h, b, slot, free, [(v, t)])
            yield from divided(u, tag, b, slot)

        def l1_attention(u, b, q_ready):
            at, c = {}, {}
            for h in range(2):
                at["ctx"] = yield from score(u, "ctx", h, b, q_ready)
                c[h, 0], free = yield Take("chunk", "vector", [("score", u, "ctx", h), ("mask_keys", u)])
                cc, ps = by_key(chunk[c[h, 0]]), by_key(scores[at["ctx"]][:, :])
                yield step("vector", 600, ("masked", u, "ctx", h), [("score", u, "ctx", h), ("mask_keys", u), free],
                           lambda e, cc=cc, ps=ps: e.tensor_tensor(cc, ps, over_heads(b.keys[:, :]), ALU.add))
                plan.free("scores", at["ctx"], ("masked", u, "ctx", h))
                yield step("vector", 600, ("max", u, "ctx", h), [("masked", u, "ctx", h)],
                           lambda e, cc=cc, h=h: e.tensor_reduce(max_of(b, 0, h), cc, AX.X, ALU.max))
                at["lat"] = yield from score(u, "lat", h, b, q_ready)
                ps = by_key(scores[at["lat"]][:, :])
                yield step("vector", 600, ("max", u, "lat", h), [("score", u, "lat", h)],
                           lambda e, ps=ps, h=h: e.tensor_reduce(max_of(b, 1, h), ps, AX.X, ALU.max))
                yield step("vector", 75, ("max", u, "both", h), [("max", u, "lat", h)],
                           lambda e, h=h: e.tensor_tensor(max_of(b, 0, h), max_of(b, 0, h), max_of(b, 1, h), ALU.max))
                yield step("gpsimd", 1000, ("shifted2", u, "ctx", h), [("max", u, "both", h)],
                           lambda e, cc=cc, h=h: e.tensor_tensor(cc, cc, over_keys(max_of(b, 0, h)), ALU.subtract))
                c[h, 1], free = yield Take("chunk", "vector", [("max", u, "both", h)])
                cl = by_key(chunk[c[h, 1]])
                yield step("vector", 600, ("shifted", u, "lat", h), [("max", u, "both", h), free],
                           lambda e, cl=cl, ps=ps, h=h: e.tensor_tensor(cl, ps, over_keys(max_of(b, 0, h)), ALU.subtract))
                plan.free("scores", at["lat"], ("shifted", u, "lat", h))
                yield step("scalar", 530, ("exp", u, "lat", h), [("shifted", u, "lat", h)],
                           lambda e, cl=cl: e.activation(cl, cl, ACT.Exp))
                yield step("scalar", 530, ("exp", u, "ctx", h), [("shifted2", u, "ctx", h)],
                           lambda e, cc=cc: e.activation(cc, cc, ACT.Exp))
            slot = None
            for h in range(2):
                tl = yield from turn_chunk(u, "lat", 1, h, b, c[h, 1], ("exp", u, "lat", h))
                tc = yield from turn_chunk(u, "lat", 0, h, b, c[h, 0], ("exp", u, "ctx", h))
                if slot is None:
                    slot, free = yield Take("mixed", "tensor", [("probT", u, "lat", i, h) for i in range(2)] + [("val", u, ("lat", i)) for i in range(2)])
                yield from mix_half(u, "lat", h, b, slot, free, [(0, tc), (1, tl)])
            yield from divided(u, "lat", b, slot)

        def mlp(u, tag, b, w1, b1, w2, ready, add, out_ap):
            at = HALVED[w1]
            c, parts = [None] * 2, [None] * 2
            for g in range(2):
                slot, free = yield Take("work", "tensor", [("x_lo", u, tag), ("lo", w1)])

                def products(e, g=g, slot=slot):
                    for j in range(4):
                        last = halved_tile(e, work[slot][:, j * P:(j + 1) * P], w1, (4 * g + j) * P, b)
                    return last
                yield step("tensor", 4 * 3 * 56 * KH, ("hid_mm", u, tag, g), [("x_lo", u, tag), ("lo", w1), free], products)
                c[g], c_free = yield Take("chunk", "scalar", [("hid_mm", u, tag, g)] + ready)

                def gelu(e, g=g, slot=slot):
                    for j in range(4):
                        last = e.activation(chunk[c[g]][:, j * P:(j + 1) * P], work[slot][:, j * P:(j + 1) * P],
                                            ACT.Gelu_apprx_tanh, bias=b1[:, 4 * g + j:4 * g + j + 1],
                                            scale=down[:, HALVED[w1]:HALVED[w1] + 1])
                    return last
                yield step("scalar", 1387, ("hid", u, tag, g), [("hid_mm", u, tag, g), c_free] + ready, gelu)
                plan.free("work", slot, ("hid", u, tag, g))
                parts[g], p_free = yield Take("chunk", "vector", [("hid", u, tag, g), ("top", "hidden_" + w1, 4)])
                both = chunk[parts[g]].bitcast(F16)
                hi, lo = both[:, 0:512], both[:, 512:1024]
                yield step("vector", 330, ("hid_hi", u, tag, g), [("hid", u, tag, g), ("top", "hidden_" + w1, 4), p_free],
                           lambda e, g=g, hi=hi: e.tensor_scalar(hi, chunk[c[g]], hidden_up[:, at:at + 1], None, ALU.mult))
                yield step("vector", 600, ("hid_lo", u, tag, g), [("hid_hi", u, tag, g)],
                           lambda e, g=g, hi=hi, lo=lo: e.scalar_tensor_tensor(lo, chunk[c[g]], hidden_up[:, at:at + 1], hi,
                                                                               ALU.mult, ALU.subtract))
                plan.free("chunk", c[g], ("hid_lo", u, tag, g))
            tiles = []
            for g in range(2):
                both = chunk[parts[g]].bitcast(F16).rearrange("p (i j t) -> p i j t", i=2, j=4)
                for j in range(4):
                    hi, lo = both[:, 0, j, :], both[:, 1, j, :]
                    w_h, w_l = w_hi[w2][:, 4 * g + j, :], w_lo[w2][:, 4 * g + j, :]
                    tiles += [(g, hi, w_h), (g, hi, w_l), (g, lo, w_h)]
            yield from projected(u, tag, tiles, {g: [("hid_lo", u, tag, g), ("lo", w2)] for g in range(2)}, add, out_ap,
                                 down[:, HALVED[w2]:HALVED[w2] + 1])
            for g in range(2):
                plan.free("chunk", parts[g], ("proj_mm", u, tag, 1))

        def from_xT(b, wt):
            return [(0, b.xT[:, k, :], wt[:, k, :]) for k in range(KH)]

        def unit(u, b):
            s = u % STREAMS
            tok = slice(u * P, (u + 1) * P)
            loaded = (f"ld_unit{s}", u)
            stored = [(f"store{s}", u - STREAMS)] if u >= STREAMS else []

            yield from normed(u, "self", b, b.xin[:, :], [loaded], L0_EPS, True)
            yield from halved_features(u, "self", "qkv", 4, b, b.qk[:, :, :], folded[:, 0:4],
                                       [("fold_add", "sq", 1), ("fold_add", "skv")])
            yield from spread_keys(u, "self", b.qk[:, KH:, :], [("feat", u, "self")], "own_keys")
            v_hi, v_lo = plain(b.x_hi, w_hi["qkv"], 2 * H), plain(b.x_lo, w_hi["qkv"], 2 * H)
            yield from values(u, ("self", 0), b, 0, v_hi + v_lo + plain(b.x_hi, w_lo["qkv"], 2 * H), [],
                              down[:, HALVED["qkv"]:HALVED["qkv"] + 1])
            yield plus_bias(u, "self", b.xb[:, :], b.xin[:, :], "b_ao", [loaded, ("through_add", "ao")] + stored)
            yield from l0_attention(u, "self", 0, b, mask_self[:, :], add_self[:, :], [("add_self",)],
                                    [("feat", u, "self")])
            yield from projected(u, "self", from_xT(b, w["ao"]), {0: [("xT", u, ("self", "heads")), ("ld_w_ao",)]},
                                 b.xb[:, :], b.x[:, :])

            yield step("vector", 140, ("mask_keys", u), [loaded],
                       lambda e: e.tensor_scalar(b.keys[:, :], b.keys_i[:, :], 0, MASKED, ALU.is_equal, ALU.mult))

            yield from normed(u, "cross", b, b.x[:, :], [("proj", u, "self")], L0_EPS, True)
            yield plus_bias(u, "cross", b.xb[:, :], b.x[:, :], "b_co", [("proj", u, "self"), ("through_add", "co")])
            yield from halved_features(u, "cross", "q", 2, b, b.qk[:, 0:KH, :], folded[:, 6:8], [("fold_add", "cq", 1)])
            yield from l0_attention(u, "cross", 1, b, b.mask[:, :], b.add[:, :], [("add_cross", u)],
                                    [("feat", u, "cross")])
            yield from projected(u, "cross", from_xT(b, w["co"]), {0: [("xT", u, ("cross", "heads")), ("ld_w_co",)]},
                                 b.xb[:, :], b.x[:, :])

            yield from normed(u, "mlp0", b, b.x[:, :], [("proj", u, "cross")], L0_EPS, True)
            yield plus_bias(u, "mlp0", b.xb[:, :], b.x[:, :], "b2", [("proj", u, "cross")])
            yield from mlp(u, "mlp0", b, "m1", folded[:, 8:16], "m2", [("fold_add", "m1")], b.xb[:, :], b.x[:, :])

            yield from turned(u, "lat", b, b.x[:, :], [("proj", u, "mlp0")])
            yield from features(u, "lat_k", [(w["lk"], 0, 2, b.xT)], b.qk[:, KH:, :], col("k_b", 0, 2),
                                [("xT", u, "lat"), ("ld_w_lk",)])
            yield from spread_keys(u, "lat", b.qk[:, KH:, :], [("feat", u, "lat_k")], "own_keys")
            yield plus_bias(u, "lat", b.xb[:, :], b.x[:, :], "out_b", [("proj", u, "mlp0"), ("through_add", "lo")])
            yield from features(u, "lat_q", [(w["lq"], 0, 2, b.xT)], b.qk[:, 0:KH, :], col("q_b", 0, 2),
                                [("scale_w", "lq"), ("scale_lqb",)])
            yield from values(u, ("lat", 1), b, 1, plain(b.xT, w["lv"]), [("ld_w_lv",)])
            yield from l1_attention(u, b, [("feat", u, "lat_q")])
            yield from projected(u, "lat", from_xT(b, w["lo"]), {0: [("xT", u, ("lat", "heads")), ("ld_w_lo",)]},
                                 b.xb[:, :], b.xb[:, :])

            yield from normed(u, "mlp1", b, b.xb[:, :], [("proj", u, "lat")], L1_EPS, False)
            yield plus_bias(u, "mlp1", b.x[:, :], b.x[:, :], "mlp_b2", [("plus_bias", u, "lat"), ("turn", u, "lat")])
            yield from mlp(u, "mlp1", b, "n1", col("mlp_b1", 0, 8), "n2", [("ld_cols",)],
                           b.x[:, :], b.xb[:, :])
            yield dma((f"store{s}", u), [("proj", u, "mlp1")], [(out[tok, :], b.xb[:, :])])

        def context(u, b):
            s, before = u % STREAMS, u - STREAMS
            tok = slice(u * P, (u + 1) * P)
            read = [] if before < 0 else [("xn", before, "self"), ("plus_bias", before, "self"),
                                          ("masked", before, "cross", 1), ("val_mm", before, ("lat", 0)), ("mask_keys", before)]
            yield dma((f"ld_unit{s}", u), read,
                      [(b.xin[:, :], x_in[tok, :]), (b.ctxT[:, :, :], ctxT_in[u]), (b.mask[:, :], mask_cross_in[tok, :])]
                      + [(b.keys_i[S * q:S * q + S, :], mask_keys_in[u * BU + q:u * BU + q + 1, :].broadcast_to([S, S]))
                         for q in range(BU)])
            loaded = (f"ld_unit{s}", u)
            mixed_before = [] if before < 0 else [("mix", before, "lat", 1)]
            yield step("gpsimd", 250, ("add_cross", u), [loaded],
                       lambda e: e.tensor_scalar(b.add[:, :], b.mask[:, :], -1.0, 10000.0, ALU.add, ALU.mult))
            yield from features(u, "cross_k", [(w["kv"], 0, 2, b.ctxT)], b.kc[:, :, :], col("b_kv", 0, 2),
                                [loaded, ("ld_w_kv",)] + mixed_before)
            yield from values(u, ("cross", 1), b, 1, plain(b.ctxT, w["kv"], H), [])
            yield from spread_keys(u, "cross", b.kc[:, :, :], [("feat", u, "cross_k"), ("score", u, "self", 0)], "ctx_keys")
            yield from features(u, "ctx_k", [(w["lk"], 0, 2, b.ctxT)], b.kc[:, :, :], col("k_b", 0, 2),
                                [("ld_w_lk",), (f"place_keys_cross{s}", u), ("score", u, "cross", 1)])
            yield from values(u, ("lat", 0), b, 0, plain(b.ctxT, w["lv"]), [("ld_w_lv",), ("mix", u, "self", 1)])
            yield from spread_keys(u, "ctx", b.kc[:, :, :], [("feat", u, "ctx_k"), ("xn", u, "mlp0")], "ctx_keys")

        def stream(s, part):
            for u in range(s, UNITS, STREAMS):
                yield from part(u, bufs[s])

        plan.weave([constants(), setup(), folds()] + [stream(s, part) for part in (unit, context) for s in range(STREAMS)])

        block = ctx.enter_context(nc.Block())

        @block.tensor
        def _(eng):
            for run in plan.queues["tensor"]:
                run(eng)

        @block.vector
        def _(eng):
            for run in plan.queues["vector"]:
                run(eng)

        @block.scalar
        def _(eng):
            for run in plan.queues["scalar"]:
                run(eng)

        @block.gpsimd
        def _(eng):
            for run in plan.queues["gpsimd"]:
                run(eng)

        @block.sync
        def _(eng):
            for run in plan.queues["sync"]:
                run(eng)
            for s in range(STREAMS):
                eng.wait_ge(plan.sems[f"store{s}"], plan.count[f"store{s}"])


def kernel(**inputs):
    import concourse.bacc as bacc
    from concourse.bass_utils import run_bass_kernel_spmd as launch

    a = {k: np.ascontiguousarray(v) for k, v in inputs.items()}
    l0 = lambda n: a["L0_xattn_" + n]
    l1 = lambda n: a["L1_xattn_" + n]

    def columns(v):
        return v.reshape(-1, P).T

    kv_w = l1("kv_w").reshape(H, H, 2)
    kv_b = l1("kv_b").reshape(H, 2)
    cols = {"ln1_s": l0("ln1_s"), "ln1_b": l0("ln1_b"), "b_qkv": l0("b_qkv"), "ln2_s": l0("ln2_s"),
            "ln2_b": l0("ln2_b"), "b_q": l0("b_q"), "b_kv": l0("b_kv"), "ln3_s": l0("ln3_s"),
            "ln3_b": l0("ln3_b"), "b1": l0("b1"), "q_b": l1("q_b"), "k_b": kv_b[:, 0], "v_b": kv_b[:, 1],
            "postnorm_w": l1("postnorm_w"), "mlp_b1": l1("mlp_b1")}
    rows = {"b_ao": l0("b_ao"), "b_co": l0("b_co"), "b2": l0("b2"), "out_b": l1("out_b"), "mlp_b2": l1("mlp_b2")}
    weights = {"qkv": l0("w_qkv"), "ao": l0("w_ao"), "q": l0("w_q"), "kv": l0("w_kv"), "co": l0("w_co"),
               "m1": l0("w1"), "m2": l0("w2"), "lq": l1("q_w"), "lk": kv_w[:, :, 0], "lv": kv_w[:, :, 1],
               "lo": l1("out_w"), "n1": l1("mlp_w1"), "n2": l1("mlp_w2")}
    arrays = {
        "x": a["x"].reshape(B * S, H),
        "ctxT": a["ctx_2048"].reshape(UNITS, P, KH, P).transpose(0, 3, 2, 1),
        "mask_self": a["mask_1x1xSxS2_fc1"].reshape(S, S),
        "mask_cross": a["mask_Bx1xSxS2_ff1"].reshape(B * S, S),
        "mask_keys": a["mask_BxS2_ik0"],
        "cols": np.concatenate([columns(cols[n]) for n in COLS], axis=1),
        "rows": np.stack([rows[n] for n in ROWS])[None],
    }
    arrays.update({"w_" + n: v for n, v in weights.items()})
    arrays = {k: np.ascontiguousarray(v) for k, v in arrays.items()}

    nc = bacc.Bacc("TRN2", target_bir_lowering=False, num_devices=1)
    d = {k: nc.dram_tensor("in_" + k, v.shape, mybir.dt.from_np(v.dtype), kind="ExternalInput").ap()
         for k, v in arrays.items()}
    out = nc.dram_tensor("out", (B * S, H), F32, kind="ExternalOutput").ap()
    build(nc, d["x"], d["ctxT"], d["mask_self"], d["mask_cross"], d["mask_keys"], d["cols"], d["rows"],
          {n: d["w_" + n] for n in weights}, out)
    r = launch(nc, [{"in_" + k: v for k, v in arrays.items()}], core_ids=[0])
    return r.results[0]["out"].reshape(B, S, H)
```
